# Optimizing a Trainium2 kernel written in Bass

```python
import numpy as np
import jax
import jax.numpy as jnp

def _softmax(x, axis=-1):
    return jax.nn.softmax(x, axis=axis)

def _gelu(x):
    return jax.nn.gelu(x, approximate=True)

def _silu(x):
    return jax.nn.silu(x)

def _sigmoid(x):
    return jax.nn.sigmoid(x)

def _layernorm(x, axis=-1, eps=1e-05):
    m = jnp.mean(x, axis=axis, keepdims=True)
    v = jnp.var(x, axis=axis, keepdims=True)
    return (x - m) / jnp.sqrt(v + eps)

def _scatter_add(tgt, idx, src, axis=0):
    return tgt.at[idx].add(src)

def _segment_sum(src, seg, n):
    return jax.ops.segment_sum(src, seg, n)
kernel_name = 'mk_xattn_ffn_d1_seqx_r8_db8a31'

def setup_inputs(seed: int=0):
    np.random.seed(seed)
    _w = jnp.asarray

    def _rec_inputs():
        import jax
        import jax.numpy as jnp
        _rk = jax.random.key(seed)
        x = 7.22e-05 + 1 * jax.random.normal(jax.random.fold_in(_rk, 1), (4, 512, 128), jnp.float32)
        _lenS = 512 - jax.random.randint(jax.random.fold_in(_rk, 7), (4,), 0, max(1, 512 // 4) + 1, jnp.int32)
        _lenS2 = 77 - jax.random.randint(jax.random.fold_in(_rk, 8), (4,), 0, max(1, 77 // 4) + 1, jnp.int32)
        _ctx_1024P = jax.random.normal(jax.random.fold_in(_rk, 11), (4, 16, 128), jnp.float32)
        _ctx_1024c = jax.random.dirichlet(jax.random.fold_in(_rk, 511), 0.3 * jnp.ones((16,), jnp.float32), (4, 77))
        _ctx_1024t = jnp.einsum('bsk,bkd->bsd', _ctx_1024c, _ctx_1024P)
        _ctx_1024t = _ctx_1024t * jax.lax.rsqrt(jnp.mean(jnp.square(_ctx_1024t)) + 1e-12) * 0.953939
        ctx_1024 = 4.13588e-05 + 0.999923 * (_ctx_1024t + 0.3 * jax.random.normal(jax.random.fold_in(_rk, 611), (4, 77, 128), jnp.float32))
        return (x, ctx_1024)
    x, ctx_1024 = _rec_inputs()

    def _L0_xattn_setup():
        import jax, jax.numpy as jnp
        import numpy as np
        D_MODEL = 128
        NUM_HEADS = 16
        HEAD_DIM = D_MODEL // NUM_HEADS

        def _split_heads(x):
            B, S, _ = x.shape
            return x.reshape(B, S, NUM_HEADS, HEAD_DIM).transpose(0, 2, 1, 3)
        key = jax.random.key(seed)
        ks = jax.random.split(key, 11)
        B, S, D = (4, 256, D_MODEL)
        scale = 1.0 / np.sqrt(D)
        return {'query': jax.random.normal(ks[0], (B, S, D), jnp.float32), 'key': jax.random.normal(ks[1], (B, S, D), jnp.float32), 'value': jax.random.normal(ks[2], (B, S, D), jnp.float32), 'Wq': jax.random.normal(ks[3], (D, D), jnp.float32) * scale, 'bq': jax.random.normal(ks[4], (D,), jnp.float32) * 0.01, 'Wk': jax.random.normal(ks[5], (D, D), jnp.float32) * scale, 'bk': jax.random.normal(ks[6], (D,), jnp.float32) * 0.01, 'Wv': jax.random.normal(ks[7], (D, D), jnp.float32) * scale, 'bv': jax.random.normal(ks[8], (D,), jnp.float32) * 0.01, 'Wo': jax.random.normal(ks[9], (D, D), jnp.float32) * scale, 'bo': jax.random.normal(ks[10], (D,), jnp.float32) * 0.01}
    _L0_xattn_all = _L0_xattn_setup()
    _L0_xattn_in = {k: v for k, v in _L0_xattn_all.items() if k in ('Wq', 'bq', 'Wk', 'bk', 'Wv', 'bv', 'Wo', 'bo')}
    del _L0_xattn_all

    def _L0_ffn_setup():
        import jax, jax.numpy as jnp
        import numpy as np
        D_MODEL = 128
        D_FF = 512
        N_EXPERTS = 8
        INIT_SCALE = 0.1

        def _trunc_normal(key, shape, std):
            return std * jax.random.truncated_normal(key, -2.0, 2.0, shape, dtype=jnp.float32)
        key = jax.random.key(seed)
        ks = jax.random.split(key, 5)
        x = jax.random.normal(ks[0], (4, 128, D_MODEL), dtype=jnp.float32)
        router_W = _trunc_normal(ks[1], (D_MODEL, N_EXPERTS), INIT_SCALE / np.sqrt(D_MODEL))
        router_b = jnp.zeros((N_EXPERTS,), dtype=jnp.float32)
        W1 = _trunc_normal(ks[2], (N_EXPERTS, D_MODEL, D_FF), INIT_SCALE / np.sqrt(D_MODEL))
        b1 = jnp.zeros((N_EXPERTS, D_FF), dtype=jnp.float32)
        W2 = _trunc_normal(ks[3], (N_EXPERTS, D_FF, D_MODEL), INIT_SCALE / np.sqrt(D_FF))
        b2 = jnp.zeros((N_EXPERTS, D_MODEL), dtype=jnp.float32)
        return {'x': x, 'router_W': router_W, 'router_b': router_b, 'W1': W1, 'b1': b1, 'W2': W2, 'b2': b2}
    _L0_ffn_all = _L0_ffn_setup()
    _L0_ffn_in = {k: v for k, v in _L0_ffn_all.items() if k in ('router_W', 'router_b', 'W1', 'b1', 'W2', 'b2')}
    del _L0_ffn_all
    return {'x': x, 'ctx_1024': ctx_1024, 'L0_xattn_Wq': _L0_xattn_in['Wq'], 'L0_xattn_bq': _L0_xattn_in['bq'], 'L0_xattn_Wk': _L0_xattn_in['Wk'], 'L0_xattn_bk': _L0_xattn_in['bk'], 'L0_xattn_Wv': _L0_xattn_in['Wv'], 'L0_xattn_bv': _L0_xattn_in['bv'], 'L0_xattn_Wo': _L0_xattn_in['Wo'], 'L0_xattn_bo': _L0_xattn_in['bo'], 'L0_ffn_router_W': _L0_ffn_in['router_W'], 'L0_ffn_router_b': _L0_ffn_in['router_b'], 'L0_ffn_W1': _L0_ffn_in['W1'], 'L0_ffn_b1': _L0_ffn_in['b1'], 'L0_ffn_W2': _L0_ffn_in['W2'], 'L0_ffn_b2': _L0_ffn_in['b2']}

def reference(x, ctx_1024, L0_xattn_Wq, L0_xattn_bq, L0_xattn_Wk, L0_xattn_bk, L0_xattn_Wv, L0_xattn_bv, L0_xattn_Wo, L0_xattn_bo, L0_ffn_router_W, L0_ffn_router_b, L0_ffn_W1, L0_ffn_b1, L0_ffn_W2, L0_ffn_b2):
    import jax
    import jax.numpy as jnp

    def _L0_xattn_ref(query, key, value, Wq, bq, Wk, bk, Wv, bv, Wo, bo):
        import jax, jax.numpy as jnp
        import numpy as np
        D_MODEL = 128
        NUM_HEADS = 16
        HEAD_DIM = D_MODEL // NUM_HEADS

        def _split_heads(x):
            B, S, _ = x.shape
            return x.reshape(B, S, NUM_HEADS, HEAD_DIM).transpose(0, 2, 1, 3)
        q = _split_heads(query @ Wq.T + bq)
        k = _split_heads(key @ Wk.T + bk)
        v = _split_heads(value @ Wv.T + bv)
        scores = jnp.einsum('bhqd,bhkd->bhqk', q, k) / np.sqrt(HEAD_DIM)
        attn = jax.nn.softmax(scores, axis=-1)
        out = jnp.einsum('bhqk,bhkd->bhqd', attn, v)
        B, H, S, Dh = out.shape
        out = out.transpose(0, 2, 1, 3).reshape(B, S, H * Dh)
        return out @ Wo.T + bo

    def _L0_ffn_ref(x, router_W, router_b, W1, b1, W2, b2):
        import jax, jax.numpy as jnp
        import numpy as np
        D_MODEL = 128
        D_FF = 512
        N_EXPERTS = 8
        INIT_SCALE = 0.1

        def _trunc_normal(key, shape, std):
            return std * jax.random.truncated_normal(key, -2.0, 2.0, shape, dtype=jnp.float32)
        logits = jnp.einsum('bsd,de->bse', x.astype(jnp.float32), router_W) + router_b
        probs = jax.nn.softmax(logits, axis=-1)
        top1 = jnp.argmax(probs, axis=-1)
        mask = jax.nn.one_hot(top1, N_EXPERTS, dtype=x.dtype)
        gates = mask * probs.astype(x.dtype)
        h = jax.nn.relu(jnp.einsum('bsd,edf->besf', x, W1) + b1[:, None, :])
        y = jnp.einsum('besf,efd->besd', h, W2) + b2[:, None, :]
        out = jnp.einsum('bse,besd->bsd', gates, y)
        return out
    x = x + _L0_xattn_ref(_layernorm(x, axis=-1), ctx_1024, ctx_1024, L0_xattn_Wq, L0_xattn_bq, L0_xattn_Wk, L0_xattn_bk, L0_xattn_Wv, L0_xattn_bv, L0_xattn_Wo, L0_xattn_bo)
    x = x + _L0_ffn_ref(_layernorm(x, axis=-1), L0_ffn_router_W, L0_ffn_router_b, L0_ffn_W1, L0_ffn_b1, L0_ffn_W2, L0_ffn_b2)
    return x

_drawn_inputs = setup_inputs


def setup_inputs(seed=0):
    import zlib

    import numpy as np

    out = dict(_drawn_inputs(seed))
    spreads = {'L0_ffn_router_b': (0.0, 0.591), 'L0_ffn_b1': (0.0, 0.8), 'L0_ffn_b2': (0.0, 0.625)}
    factors = {'L0_xattn_bq': 8.0,
     'L0_xattn_bk': 8.0,
     'L0_xattn_bv': 5.57,
     'L0_xattn_bo': 5.601,
     'L0_ffn_router_W': 5.423,
     'L0_ffn_W1': 8.0,
     'L0_ffn_W2': 8.0}
    for name, (base, spread) in spreads.items():
        noise = np.random.default_rng([zlib.crc32(name.encode()), seed]).standard_normal(out[name].shape)
        drawn = base * np.exp(spread * noise) if base else spread * noise
        out[name] = jnp.asarray(drawn.astype(out[name].dtype))
    for name, factor in factors.items():
        out[name] = (out[name] * factor).astype(out[name].dtype)
    return out
```

```python
import concourse.bass as bass
from concourse import mybir
from contextlib import ExitStack

P = 128
BATCH, SEQ, D = 4, 512, 128
CTX = 77
HEADS, DH = 16, 8
GROUPS = 4
GH = HEADS // GROUPS
GK = GH * CTX
CHUNKS = -(-GK // P)
GKP = CHUNKS * P
EXPERTS, FF = 8, 512
FC = FF // P
TT = SEQ // P
TILES = BATCH * TT
PAGES = TILES + EXPERTS - 1
STEPS = (PAGES + 1) // 2
ROW = 2 * D + 2
REST = ROW - D
NO_TOKEN = BATCH * SEQ
EPS = 1e-5
SCALE = float(DH) ** -0.5

C_ID, C_LT, C_ONE = 0, P, 2 * P
C_HM = 3 * P
C_MC = C_HM + GH
C_ON = C_MC + CHUNKS * GROUPS * GH
C_REV = C_ON + CHUNKS * 32
C_PG = C_REV + EXPERTS
C_SL = C_PG + TILES
C_TOK = C_SL + PAGES
C_NH = C_TOK + TILES
CC = C_NH + 4


def layer(nc, x, ctx, Wq, bq, Wk, bk, Wv, bv, Wo, bo, rW, rb, W1, b1, W2, b2, cst, sel, out):
    f32, f32r, i32 = mybir.dt.float32, mybir.dt.float32r, mybir.dt.int32
    ALU, ACT, AX = mybir.AluOpType, mybir.ActivationFunctionType, mybir.AxisListType

    x_v = x.rearrange("b (t p) d -> b p t d", p=P)
    out_rows = out.rearrange("b s d -> (b s) d")
    slots = nc.dram_tensor("slots", [PAGES * P, ROW], f32, kind="Internal").ap()

    with ExitStack() as es:
        def sb(name, shape, dt=f32):
            return es.enter_context(nc.sbuf_tensor(name, shape, dt))

        def sem(name):
            return es.enter_context(nc.semaphore(name))

        cs = sb("cs", [P, CC])
        ident, ltri, ones = cs[:, C_ID:C_ID + P], cs[:, C_LT:C_LT + P], cs[:, C_ONE:C_ONE + P]
        head_mask = cs[:, C_HM:C_HM + GH]
        row_mask = cs[:, C_MC:C_ON].rearrange("p (m h) -> p m h", h=GH)
        ones_mask = cs[:, C_ON:C_REV].rearrange("p (c m) -> p c m", m=32)
        rev, page_edges = cs[:, C_REV:C_REV + EXPERTS], cs[:, C_PG:C_PG + TILES]
        page_no, token_no = cs[:, C_SL:C_SL + PAGES], cs[:, C_TOK:C_TOK + TILES]
        neg_half = cs[:, C_NH:C_NH + 4]
        selr = sb("selr", [P, GROUPS * CHUNKS, P], f32r)
        w_in = sb("w_in", [P, 4, D])
        wq_rep, wk_rep = sb("wq_rep", [P, GROUPS, 4, 32]), sb("wk_rep", [P, GROUPS, 4, 32])
        wvT, woT = sb("wvT", [P, D]), sb("woT", [P, D])
        b_in, b_cols = sb("b_in", [2 * GROUPS + 1, D]), sb("b_cols", [P, 2 * GROUPS + 1])
        bq_rep, bk_rep, bv_col = b_cols[:, 0:GROUPS], b_cols[:, GROUPS:2 * GROUPS], b_cols[:, 2 * GROUPS:2 * GROUPS + 1]
        bv_bc = sb("bv_bc", [P, P])
        bo_bc, bo2 = sb("bo_bc", [P, D]), sb("bo2", [P, D])
        rw_sb, rb_bc = sb("rw_sb", [P, EXPERTS]), sb("rb_bc", [P, EXPERTS])
        w1_sb, w2_sb = sb("w1_sb", [P, EXPERTS * FF]), sb("w2_sb", [P, EXPERTS * FC * D])
        b1_bc, b2_bc = sb("b1_bc", [P, EXPERTS * FF]), sb("b2_bc", [P, EXPERTS * D])
        ctx_in = sb("ctx_in", [CTX, BATCH, D])
        ctxT = sb("ctxT", [P, BATCH, 5, CTX])
        k_parts = sb("k_parts", [P, GROUPS, BATCH, CTX])
        k_parts_r = k_parts
        k_blk = sb("k_blk", [P, BATCH, GROUPS, GKP], f32r)
        v_blk = sb("v_blk", [P, BATCH, CHUNKS * GROUPS, GH, DH])
        tokens = sb("tokens", [P, (TILES + 2 * TT) * D])
        x_in = tokens[:, 0:TILES * D].rearrange("p (t d) -> p t d", d=D)
        xb = tokens[:, TILES * D:].rearrange("p (b t d) -> p b t d", b=2, d=D)
        pg_rest = tokens[:, 0:PAGES * REST].rearrange("p (s r) -> p s r", r=REST)
        st1, mv1 = sb("st1", [P, TILES, 6]), sb("mv1", [P, TILES, 2])
        st2, mv2 = sb("st2", [P, TILES, 6]), sb("mv2", [P, TILES, 2])
        rstd, shift = sb("rstd", [P, 2, TILES]), sb("shift", [P, 2, TILES])
        xn = sb("xn", [P, 2, TT, D])
        xnT = sb("xnT", [P, SEQ])
        q_parts = sb("q_parts", [P, 2, GROUPS, SEQ], f32r)
        nmax = sb("nmax", [P, TT, HEADS])
        nmax_parts = sb("nmax_parts", [P, TT, 2 * HEADS], f32r)
        nmaxT = sb("nmaxT", [P, 2, SEQ], f32r)
        probs = sb("probs", [P, 2, GROUPS, SEQ])
        rden = sb("rden", [P, SEQ])
        attnT = sb("attnT", [P, SEQ])
        rows = sb("rows", [P, TILES, ROW])
        xn2T = sb("xn2T", [P, SEQ])
        lg, ex = sb("lg", [P, TT, EXPERTS]), sb("ex", [P, TT, EXPERTS])
        one_hot = sb("one_hot", [P, TT, EXPERTS])
        before = sb("before", [P, TT + 1, EXPERTS])
        mx, den = sb("mx", [P, TT]), sb("den", [P, TT])
        rank = sb("rank", [P, TT, EXPERTS])
        offs = sb("offs", [P, TT, EXPERTS])
        total = sb("total", [P, 2, EXPERTS])
        cmp_pg = sb("cmp_pg", [P, EXPERTS, TILES])
        npages = sb("npages", [P, 2, EXPERTS])
        fresh = sb("fresh", [P, EXPERTS])
        ends = sb("ends", [P, BATCH + 1, EXPERTS])
        edge, move, base = sb("edge", [P, EXPERTS]), sb("move", [P, EXPERTS]), sb("base", [P, EXPERTS])
        slot_no = sb("slot_no", [P, TILES], i32)
        cmp_ex = sb("cmp_ex", [P, PAGES, EXPERTS])
        owner = sb("owner", [P, PAGES])
        page_ex = sb("page_ex", [P, 2 * STEPS + 2])
        page_exi = sb("page_exi", [P, STEPS, 4], i32)
        empty = sb("empty", [P, ROW])
        pg = sb("pg", [P, 2, D])
        pgT = sb("pgT", [P, 2, P])
        sel_f = probs[0:32, 1].rearrange("p g s -> p (g s)")[:, 0:GROUPS * CHUNKS * P].rearrange("p (m r) -> p m r", r=P)
        hid, hidT = probs[:, 0, 0:2, :], probs[:, 0, 2:4, :]
        y_sb = sb("y_sb", [P, 2, D])
        out_sb = sb("out_sb", [P, 2, D])
        gate_tok = sb("gate_tok", [P, 2, 2])

        def pb(name, banks):
            return es.enter_context(nc.psum_tensor(name, [P, banks, 512], f32))
        sc = pb("sc", 4)
        mi = pb("mi", 2)
        ol = pb("ol", 2)

        ld_cst, ld_w, ld_ctx, ld_bias, ld_sel = (sem(n) for n in ("ld_cst", "ld_w", "ld_ctx", "ld_bias", "ld_sel"))
        ld_x = [sem(f"ld_x{b}") for b in range(BATCH)]
        ld_ffn = sem("ld_ffn")
        slots_empty = sem("slots_empty")
        wT_done, ctxT_done, w_kept, ctx_kept = sem("wT_done"), sem("ctxT_done"), sem("w_kept"), sem("ctx_kept")
        k_done, k_hi_kept, k_kept, k_blk_kept = sem("k_done"), sem("k_hi_kept"), sem("k_kept"), sem("k_blk_kept")
        v_done, v_kept, bo2_kept = sem("v_done"), sem("v_kept"), sem("bo2_kept")
        pads_zero, sel_kept, bv_kept = sem("pads_zero"), sem("sel_kept"), sem("bv_kept")
        b_kept = sem("b_kept")
        ln1_stats, xn_kept, xb_kept = sem("ln1_stats"), sem("xn_kept"), sem("xb_kept")
        ln2_stats, xn2_kept = sem("ln2_stats"), sem("xn2_kept")
        mi_filled = sem("mi_filled")
        mi_act = sem("mi_act")
        mi_dve = sem("mi_dve")
        q_hi_kept = sem("q_hi_kept")
        nmax_split = sem("nmax_split")
        sc_filled, exp_done = sem("sc_filled"), sem("exp_done")
        sums_done = sem("sums_done")
        attn_kept, scatters = sem("attn_kept"), sem("scatters")
        shifted, ex_kept = sem("shifted"), sem("ex_kept")
        one_hot_kept = sem("one_hot_kept")
        routed, sent = sem("routed"), sem("sent")
        experts_kept = sem("experts_kept")
        pool_step, dve_step = sem("pool_step"), sem("dve_step")
        rest_loaded = sem("rest_loaded")
        pg_loaded = [sem("pg_loaded0"), sem("pg_loaded1")]
        pgT_done, pgT_kept = sem("pgT_done"), sem("pgT_kept")
        up_done, hid_kept = sem("up_done"), sem("hid_kept")
        hidT_done, hidT_kept = sem("hidT_done"), sem("hidT_kept")
        down_done, y_kept, out_kept = sem("down_done"), sem("y_kept"), sem("out_kept")
        tok_kept = sem("tok_kept")
        written = [sem("written0"), sem("written1")]

        REST_CUTS = [(0, 2), (2, 8), (8, PAGES)]

        JOBS = [("w", 0, 0), ("c", 0, 0)]
        JOBS += [("xT", 0, 0)] + [("q", 0, g) for g in range(GROUPS)]
        JOBS += [("v", b, 0) for b in range(2, BATCH)]
        JOBS += [("a", 0, i) for i in range(TT * GROUPS)] + [("mT", 0, 0)]
        for b in range(BATCH):
            n = b + 1
            if b:
                JOBS += [("y", b - 1, 0)]
            if n < BATCH:
                JOBS += [("xT", n, 0)] + [("q", n, g) for g in range(GROUPS)] + [("a", n, i) for i in range(GROUPS)]
            if b:
                JOBS += [("x2T", b - 1, 0), ("lg", b - 1, 0)]
            if n < BATCH:
                JOBS += [("a", n, i) for i in range(GROUPS, TT * GROUPS)] + [("mT", n, 0)]
            if b:
                JOBS += [("rk", b - 1, 0)]
        JOBS += [(k, BATCH - 1, 0) for k in ("y", "x2T", "lg", "rk")]
        BY_ACT = ("w", "c", "xT", "mT", "x2T")

        def read_count(i):
            act = JOBS[i][0] in BY_ACT
            return sum((j[0] in BY_ACT) == act for j in JOBS[:i + 1])

        def job(kind, b=0, i=0):
            return JOBS.index((kind, b, i))

        def load_experts(eng, s):
            row = page_exi[0:1, s // 2, :] if isinstance(s, int) else \
                page_exi[0:1].rearrange("p i j -> p (i j)")[:, bass.ds(s * 2, 4)]
            return nc.values_load_multi_w_load_instructions(
                row, engines=(eng.engine,), min_val=0, max_val=EXPERTS - 1,
                skip_runtime_bounds_check_because="the table is clamped to the experts' numbers")[1]

        def mi_take(pe, kind, b=0, i=0):
            n = job(kind, b, i)
            if n >= 2:
                pe.wait_ge(mi_act if JOBS[n - 2][0] in BY_ACT else mi_dve, read_count(n - 2))
            return mi[:, n % 2]

        def mi_wait(eng, kind, b=0, i=0):
            n = job(kind, b, i)
            eng.wait_ge(mi_filled, n + 1)
            return mi[:, n % 2]

        block = es.enter_context(nc.Block())

        @block.sync
        def _(sp):
            sp.dma_start(cs[:, :], cst).then_inc(ld_cst, 16)
            for i, w in enumerate((Wq, Wk, Wv, Wo)):
                sp.dma_start(w_in[:, i, :], w).then_inc(ld_w, 16)
            for b in range(1, BATCH):
                sp.dma_start(x_in[:, b * TT:(b + 1) * TT, :], x_v[b]).then_inc(ld_x[b], 16)
            sp.dma_start(rw_sb[:, :], rW).then_inc(ld_ffn, 16)
            sp.dma_start(rb_bc[:, :], rb.unsqueeze(0).to_broadcast([P, EXPERTS])).then_inc(ld_ffn, 16)
            sp.wait_ge(pads_zero, 5)
            sp.dma_start(slots.rearrange("(s p) r -> p s r", p=P),
                         empty[:, :].unsqueeze(1).to_broadcast([P, PAGES, ROW])).then_inc(slots_empty, 16)
            sp.dma_start(w1_sb[:, :].rearrange("p (e f) -> p e f", e=EXPERTS),
                         W1.rearrange("e d f -> d e f")).then_inc(ld_ffn, 16)
            sp.dma_start(w2_sb[:, :].rearrange("p (e d) -> p e d", d=D),
                         W2.rearrange("e (c p) d -> p (e c) d", p=P)).then_inc(ld_ffn, 16)
            sp.dma_start(b1_bc[:, :], b1.rearrange("e f -> (e f)").unsqueeze(0).to_broadcast([P, EXPERTS * FF])).then_inc(ld_ffn, 16)
            sp.dma_start(b2_bc[:, :], b2.rearrange("e d -> (e d)").unsqueeze(0).to_broadcast([P, EXPERTS * D])).then_inc(ld_ffn, 16)

            sp.wait_ge(sent, 16 * TILES)
            slots_v = slots.rearrange("(s p) r -> s p r", p=P)
            for k in range(2):
                sp.dma_start(pg[:, k, :], slots_v[k, :, 0:D]).then_inc(pg_loaded[k], 16)
            for i, (s0, s1) in enumerate(REST_CUTS):
                sp.dma_start(pg_rest[:, s0:s1, :], slots_v[s0:s1, :, D:ROW].rearrange("s p r -> p s r")).then_inc(rest_loaded, 16)

            def load(s, k):
                sp.wait_ge(pgT_done, s + 1)
                sp.dma_start(pg[:, k, :], slots_v[bass.ds(s + 2, 1), :, 0:D].rearrange("s p r -> (s p) r")).then_inc(pg_loaded[k], 16)

            with sp.Fori(0, PAGES - 3, 2) as s:
                load(s, 0)
                load(s + 1, 1)
            load(PAGES - 3, 0)

        @block.gpsimd
        def _(pool):
            steps = [0]

            def link(ins):
                steps[0] += 1
                ins.then_inc(pool_step, 1)
                pool.wait_ge(pool_step, steps[0])

            nc.gpsimd.memset(k_blk[:, :, :, GK:GKP].bitcast(f32), 0.0).then_inc(pads_zero, 1)
            nc.gpsimd.memset(nmaxT[:, :, :].bitcast(f32), 0.0).then_inc(pads_zero, 1)
            nc.gpsimd.memset(selr[:, :, :].bitcast(f32), 0.0).then_inc(pads_zero, 1)
            nc.gpsimd.memset(empty[:, 0:ROW - 1], 0.0).then_inc(pads_zero, 1)
            nc.gpsimd.memset(empty[:, ROW - 1:ROW].bitcast(i32), NO_TOKEN).then_inc(pads_zero, 1)
            nc.gpsimd.memset(before[:, 0, :], 0.0).then_inc(pads_zero, 1)
            pool.wait_ge(pads_zero, 3)
            pool.wait_ge(ld_sel, 16)
            nc.gpsimd.tensor_copy(selr[0:32, :, :], sel_f[:, :, :]).then_inc(sel_kept, 1)
            pool.wait_ge(ld_cst, 16)
            nc.gpsimd.tensor_copy(rows[:, :, ROW - 1].bitcast(i32), token_no.bitcast(i32)).then_inc(sel_kept, 1)

            def norm(which, mv, b, src, dst, signal):
                t0 = b * TT
                r, s = rstd[:, which, t0:t0 + TT], shift[:, which, t0:t0 + TT]
                link(nc.gpsimd.tensor_scalar(s, mv[:, t0:t0 + TT, 1], EPS, 1.0, ALU.add, ALU.mult))
                link(nc.gpsimd.tensor_tensor(r, s, neg_half, ALU.pow))
                link(nc.gpsimd.tensor_tensor(s, mv[:, t0:t0 + TT, 0], r, ALU.mult))
                link(nc.gpsimd.tensor_scalar(s, s, -1.0, 0.0, ALU.mult, ALU.add))
                for t in range(TT):
                    nc.gpsimd.tensor_scalar(dst(t), src(t), rstd[:, which, t0 + t:t0 + t + 1],
                                            shift[:, which, t0 + t:t0 + t + 1], ALU.mult, ALU.add).then_inc(signal, 1)

            def ln1(b):
                pool.wait_ge(ln1_stats, b + 1)
                if b >= 2:
                    pool.wait_ge(mi_filled, job("xT", b - 2) + 1)
                norm(0, mv1, b, lambda t: x_in[:, b * TT + t, :], lambda t: xn[:, b % 2, t, :], xn_kept)

            def x_plus_bias(b):
                pool.wait_ge(bo2_kept, 1)
                if b >= 2:
                    pool.wait_ge(mi_dve, read_count(job("y", b - 2)))
                nc.gpsimd.tensor_tensor(xb[:, b % 2], x_in[:, b * TT:(b + 1) * TT, :],
                                        bo2[:, :].unsqueeze(1).to_broadcast([P, TT, D]), ALU.add).then_inc(xb_kept, 1)

            def k_block(b):
                if b == 1:
                    pool.wait_ge(k_kept, 2 * GROUPS)
                    pool.wait_ge(k_hi_kept, GROUPS)
                for g in range(GROUPS):
                    nc.gpsimd.tensor_tensor(k_blk[:, b, g, 0:GK].rearrange("p (h k) -> p h k", k=CTX),
                                            k_parts[:, g, b, :].unsqueeze(1).to_broadcast([P, GH, CTX]),
                                            head_mask.unsqueeze(2).to_broadcast([P, GH, CTX]),
                                            ALU.mult).then_inc(k_blk_kept, 1)

            def send(b):
                if b == 0:
                    pool.wait_ge(slots_empty, 16)
                    pool.wait_ge(sel_kept, 2)
                pool.wait_ge(routed, b + 1)
                for t in range(b * TT, (b + 1) * TT):
                    pool.indirect_dma_start(slots, bass.IndirectOffsetOnAxis(ap=slot_no[:, t:t + 1], axis=0),
                                            rows[:, t, :], None).then_inc(sent, 16)

            ln1(0)
            k_block(1)
            ln1(1)
            x_plus_bias(0)
            x_plus_bias(1)
            for b in range(BATCH):
                if b >= 1:
                    pool.wait_ge(ln2_stats, b)
                    norm(1, mv2, b - 1, lambda t: rows[:, (b - 1) * TT + t, D:2 * D],
                         lambda t: rows[:, (b - 1) * TT + t, 0:D], xn2_kept)
                if b + 2 < BATCH:
                    k_block(b + 2)
                    ln1(b + 2)
                    x_plus_bias(b + 2)
                if b >= 1:
                    send(b - 1)
            pool.wait_ge(ln2_stats, BATCH)
            norm(1, mv2, BATCH - 1, lambda t: rows[:, (BATCH - 1) * TT + t, D:2 * D],
                 lambda t: rows[:, (BATCH - 1) * TT + t, 0:D], xn2_kept)
            send(BATCH - 1)

            last_token = pool.to_reg(NO_TOKEN - 1)

            def scatter(s, k):
                pool.wait_ge(out_kept, s + 1)
                pool.sem_inc(scatters, 1)
                pool.indirect_dma_start(out_rows, bass.IndirectOffsetOnAxis(ap=gate_tok[:, k, 1:2].bitcast(i32), axis=0),
                                        out_sb[:, k, :], None, bounds_check=last_token,
                                        oob_is_err=False).then_inc(written[k], 16)

            with pool.Fori(0, PAGES - 1, 2) as s:
                scatter(s, 0)
                scatter(s + 1, 1)
            scatter(PAGES - 1, 0)
            pool.wait_ge(written[0], 16 * ((PAGES + 1) // 2))
            pool.wait_ge(written[1], 16 * (PAGES // 2))

        @block.scalar
        def _(act):
            act.dma_start(x_in[:, 0:TT, :], x_v[0]).then_inc(ld_x[0], 16)
            act.dma_start(ctx_in[:, :, :], ctx.rearrange("b k d -> k b d")).then_inc(ld_ctx, 16)
            act.dma_start(sel_f[:, :, :], sel).then_inc(ld_sel, 16)
            for i, bias in enumerate((bq, bk)):
                act.dma_start(b_in[i * GROUPS:(i + 1) * GROUPS, :].rearrange("g (c r) -> g c r", r=32),
                              bias.rearrange("(g r) -> g r", r=32).unsqueeze(1).to_broadcast([GROUPS, 4, 32])).then_inc(ld_bias, 16)
            act.dma_start(b_in[2 * GROUPS:2 * GROUPS + 1, :], bv.unsqueeze(0)).then_inc(ld_bias, 16)
            act.dma_start(bo_bc[:, :], bo.unsqueeze(0).to_broadcast([P, D])).then_inc(ld_bias, 16)

            m = mi_wait(act, "w")
            for i, w in enumerate((wq_rep, wk_rep)):
                nc.scalar.activation(w[:, :, :, :], m[:, i * D:(i + 1) * D].rearrange("p (g r) -> p g r", r=32)
                                     .unsqueeze(2).to_broadcast([P, GROUPS, 4, 32]), ACT.Copy).then_inc(w_kept, 1)
            nc.scalar.activation(wvT[:, :], m[:, 2 * D:3 * D], ACT.Copy).then_inc(w_kept, 1)
            nc.scalar.activation(woT[:, :], m[:, 3 * D:4 * D], ACT.Copy).then_inc(mi_act, 1)
            m = mi_wait(act, "c")
            nc.scalar.activation(b_cols[:, :], m[:, BATCH * CTX:BATCH * CTX + 2 * GROUPS + 1], ACT.Copy).then_inc(b_kept, 1)
            nc.scalar.activation(ctxT[:, :, :, :], m[:, 0:BATCH * CTX].rearrange("p (b k) -> p b k", k=CTX)
                                 .unsqueeze(2).to_broadcast([P, BATCH, 5, CTX]), ACT.Copy).then_inc(mi_act, 1)
            act.wait_ge(b_kept, 1)
            nc.scalar.activation(bv_bc[:, :], bv_col.to_broadcast([P, P]), ACT.Copy).then_inc(bv_kept, 1)
            for g in range(GROUPS):
                act.wait_ge(k_done, g + 1)
                nc.scalar.activation(k_parts[:, g].rearrange("p b k -> p (b k)").bitcast(f32r), sc[:, g, 0:BATCH * CTX],
                                     ACT.Identity, bias=bk_rep[:, g:g + 1]).then_inc(k_hi_kept, 1)

            def keep_xT(b):
                m = mi_wait(act, "xT", b)
                if b:
                    act.wait_ge(mi_filled, job("q", b - 1, GROUPS - 1) + 1)
                nc.scalar.activation(xnT[:, :], m, ACT.Copy).then_inc(mi_act, 1)

            def q_hi(b, g):
                m = mi_wait(act, "q", b, g)
                if b >= 2:
                    act.wait_ge(sc_filled, 2 * CHUNKS * (b - 1))
                nc.scalar.activation(q_parts[:, b % 2, g, :], m, ACT.Identity,
                                     bias=bq_rep[:, g:g + 1]).then_inc(q_hi_kept, 1)

            def keep_maxT(b):
                if b == 0:
                    act.wait_ge(pads_zero, 2)
                m = mi_wait(act, "mT", b)
                if b >= 2:
                    act.wait_ge(sc_filled, 2 * CHUNKS * (b - 1))
                nc.scalar.activation(nmaxT[0:2 * HEADS, b % 2, :], m[0:2 * HEADS, :], ACT.Copy).then_inc(mi_act, 1)

            def exps(b, c):
                n = b * CHUNKS + c
                if n >= 2:
                    act.wait_ge(sums_done, n - 1)
                for j in range(2):
                    act.wait_ge(sc_filled, 2 * n + j + 1)
                    nc.scalar.activation(probs[:, n % 2, 2 * j:2 * j + 2, :], sc[:, 2 * j:2 * j + 2, :], ACT.Exp,
                                         scale=SCALE).then_inc(exp_done, 1)

            def keep_x2T(b):
                m = mi_wait(act, "x2T", b)
                if b:
                    act.wait_ge(mi_filled, job("lg", b - 1) + 1)
                nc.scalar.activation(xn2T[:, :], m, ACT.Copy).then_inc(mi_act, 1)

            def gate_exp(b):
                act.wait_ge(shifted, b + 1)
                nc.scalar.activation(ex[:, :, :], ex[:, :, :], ACT.Exp).then_inc(ex_kept, 1)

            keep_xT(0)
            for g in range(GROUPS):
                q_hi(0, g)
            keep_maxT(0)
            for b in range(BATCH):
                n = b + 1
                exps(b, 0)
                if n < BATCH:
                    keep_xT(n)
                    q_hi(n, 0)
                    q_hi(n, 1)
                exps(b, 1)
                if n < BATCH:
                    q_hi(n, 2)
                    q_hi(n, 3)
                if b:
                    keep_x2T(b - 1)
                exps(b, 2)
                if b:
                    gate_exp(b - 1)
                if n < BATCH:
                    keep_maxT(n)
            keep_x2T(BATCH - 1)
            gate_exp(BATCH - 1)

            def relu(s, k):
                act.wait_ge(hidT_done, s + 1)
                nc.scalar.activation(hidT[:, k, :], ol[:, k, :], ACT.Relu).then_inc(hidT_kept, 1)

            relu(0, 0)
            with act.Fori(1, PAGES - 1, 2) as s:
                relu(s, 1)
                relu(s + 1, 0)

        @block.tensor
        def _(pe):
            pe.wait_ge(ld_cst, 16)
            pe.wait_ge(ld_w, 64)
            m = mi_take(pe, "w")
            for i in range(4):
                last = nc.tensor.transpose(m[:, i * D:(i + 1) * D], w_in[:, i, :], ident)
            last.then_inc(mi_filled, 1)
            pe.wait_ge(ld_ctx, 16)
            m = mi_take(pe, "c")
            pe.wait_ge(ld_bias, 64)
            nc.tensor.transpose(m[:, BATCH * CTX:BATCH * CTX + 2 * GROUPS + 1], b_in[:, :],
                                ident[0:2 * GROUPS + 1, 0:2 * GROUPS + 1])
            for b in range(BATCH):
                last = nc.tensor.transpose(m[:, b * CTX:(b + 1) * CTX], ctx_in[:, b, :], ident[0:CTX, 0:CTX])
            last.then_inc(mi_filled, 1)

            def transpose_x(b):
                pe.wait_ge(xn_kept, TT * (b + 1))
                m = mi_take(pe, "xT", b)
                for t in range(TT):
                    last = nc.tensor.transpose(m[:, t * P:(t + 1) * P], xn[:, b % 2, t, :], ident)
                last.then_inc(mi_filled, 1)

            def project_q(b, g):
                if g == 0:
                    pe.wait_ge(mi_act, read_count(job("xT", b)))
                m = mi_take(pe, "q", b, g)
                nc.tensor.matmul(m, wq_rep[:, g].rearrange("p c r -> p (c r)"), xnT[:, :],
                                 start=True, stop=True).then_inc(mi_filled, 1)

            def scores_for_max(b, t):
                if t == 0:
                    pe.wait_ge(mi_dve, read_count(job("q", b, GROUPS - 1)))
                    pe.wait_ge(k_blk_kept, GROUPS * (b + 1))
                for g in range(GROUPS):
                    m = mi_take(pe, "a", b, t * GROUPS + g)
                    nc.tensor.matmul(m[:, 0:GK], q_parts[:, b % 2, g, t * P:(t + 1) * P], k_blk[:, b, g, 0:GK],
                                     start=True, stop=True).then_inc(mi_filled, 1)

            def transpose_max(b):
                pe.wait_ge(nmax_split, b + 1)
                m = mi_take(pe, "mT", b)
                for t in range(TT):
                    last = nc.tensor.transpose(m[0:2 * HEADS, t * P:(t + 1) * P], nmax_parts[:, t, :].bitcast(f32), ident)
                last.then_inc(mi_filled, 1)

            def scores(b, c):
                if c == 0:
                    pe.wait_ge(mi_act, read_count(job("mT", b)))
                    if b == 0:
                        pe.wait_ge(sel_kept, 1)
                        pe.wait_ge(pads_zero, 3)
                for j in range(2):
                    n = 2 * (b * CHUNKS + c) + j
                    if n >= 2:
                        pe.wait_ge(exp_done, n - 1)
                    for g in (2 * j, 2 * j + 1):
                        nc.tensor.matmul(sc[:, g, :], k_blk[:, b, g, c * P:(c + 1) * P], q_parts[:, b % 2, g, :],
                                         start=True, stop=False)
                        last = nc.tensor.matmul(sc[:, g, :], selr[:, g * CHUNKS + c, :], nmaxT[:, b % 2, :],
                                                start=False, stop=True)
                    last.then_inc(sc_filled, 1)

            def weighted_sums(b, c):
                n = b * CHUNKS + c
                pe.wait_ge(exp_done, 2 * (n + 1))
                if n == 0:
                    pe.wait_ge(v_kept, 2)
                    pe.wait_ge(mi_dve, read_count(job("v", BATCH - 1)))
                if c == 0 and b:
                    pe.wait_ge(attn_kept, b)
                for g in range(GROUPS):
                    r = slice(32 * g, 32 * g + 32)
                    nc.tensor.matmul(ol[r, 0, :], v_blk[:, b, c * GROUPS + g].rearrange("p h d -> p (h d)"),
                                     probs[:, n % 2, g, :], start=(c == 0), stop=(c == CHUNKS - 1))
                for g in range(GROUPS):
                    r = slice(32 * g, 32 * g + 32)
                    last = nc.tensor.matmul(ol[r, 1, :], ones_mask[:, c, :], probs[:, n % 2, g, :],
                                            start=(c == 0), stop=(c == CHUNKS - 1))
                last.then_inc(sums_done, 1)

            def project_out(b):
                pe.wait_ge(attn_kept, b + 1)
                m = mi_take(pe, "y", b)
                for t in range(TT):
                    last = nc.tensor.matmul(m[:, t * D:(t + 1) * D], attnT[:, t * P:(t + 1) * P], woT[:, :],
                                            start=True, stop=True)
                last.then_inc(mi_filled, 1)

            def transpose_x2(b):
                pe.wait_ge(xn2_kept, TT * (b + 1))
                m = mi_take(pe, "x2T", b)
                for t in range(TT):
                    last = nc.tensor.transpose(m[:, t * P:(t + 1) * P], rows[:, b * TT + t, 0:D], ident)
                last.then_inc(mi_filled, 1)

            def logits(b):
                pe.wait_ge(mi_act, read_count(job("x2T", b)))
                if b == 0:
                    pe.wait_ge(ld_ffn, 96)
                m = mi_take(pe, "lg", b)
                for t in range(TT):
                    last = nc.tensor.matmul(m[:, t * EXPERTS:(t + 1) * EXPERTS], xn2T[:, t * P:(t + 1) * P], rw_sb[:, :],
                                            start=True, stop=True)
                last.then_inc(mi_filled, 1)

            def ranks(b):
                pe.wait_ge(one_hot_kept, b + 1)
                m = mi_take(pe, "rk", b)
                w = TT * EXPERTS
                nc.tensor.matmul(m[:, 0:w], ltri, one_hot[:, :, :].rearrange("p t e -> p (t e)"), start=True, stop=False)
                nc.tensor.matmul(m[:, 0:w], ones, before[:, 0:TT, :].rearrange("p t e -> p (t e)"), start=False, stop=True)
                nc.tensor.matmul(m[:, w:w + EXPERTS], ones, before[:, TT, :], start=True, stop=True).then_inc(mi_filled, 1)

            pe.wait_ge(w_kept, 3)
            pe.wait_ge(mi_act, 2)
            for g in range(GROUPS):
                nc.tensor.matmul(sc[:, g, 0:BATCH * CTX], wk_rep[:, g].rearrange("p c r -> p (c r)"),
                                 ctxT[:, :, 0, :], start=True, stop=True).then_inc(k_done, 1)
            transpose_x(0)
            pe.wait_ge(bv_kept, 1)

            def values(m, b):
                for c in range(CHUNKS):
                    last = nc.tensor.matmul(m[:, c * D:(c + 1) * D],
                                            ctxT[:, b].rearrange("p r k -> p (r k)")[:, c * P:(c + 1) * P],
                                            wvT[:, :], start=True, stop=True)
                return last

            values(ol[:, 0, :], 0).then_inc(v_done, 1)
            values(ol[:, 1, :], 1)
            nc.tensor.matmul(ol[:, 1, CHUNKS * D:(CHUNKS + 1) * D], bv_bc[:, :], woT[:, :],
                             start=True, stop=True).then_inc(v_done, 1)
            for g in range(GROUPS):
                project_q(0, g)
            for b in range(2, BATCH):
                values(mi_take(pe, "v", b), b).then_inc(mi_filled, 1)
            for t in range(TT):
                scores_for_max(0, t)
            transpose_max(0)
            for b in range(BATCH):
                n = b + 1
                scores(b, 0)
                if b:
                    project_out(b - 1)
                if n < BATCH:
                    transpose_x(n)
                    for g in range(GROUPS):
                        project_q(n, g)
                scores(b, 1)
                weighted_sums(b, 0)
                if n < BATCH:
                    scores_for_max(n, 0)
                if b:
                    transpose_x2(b - 1)
                    logits(b - 1)
                scores(b, 2)
                weighted_sums(b, 1)
                if n < BATCH:
                    scores_for_max(n, 1)
                    scores_for_max(n, 2)
                weighted_sums(b, 2)
                if n < BATCH:
                    scores_for_max(n, 3)
                    transpose_max(n)
                if b:
                    ranks(b - 1)
            project_out(BATCH - 1)
            transpose_x2(BATCH - 1)
            logits(BATCH - 1)
            ranks(BATCH - 1)

            pe.wait_ge(ld_ffn, 96)
            pe.wait_ge(experts_kept, 2)

            def transpose_page(s, k):
                pe.wait_ge(pg_loaded[k], 16 * (s // 2 + 1) if isinstance(s, int) else 8 * (s + 2 - k))
                nc.tensor.transpose(mi[:, k, 0:P], pg[:, k, :], ident).then_inc(pgT_done, 1)

            def transpose_hidden(s, k):
                pe.wait_ge(hid_kept, s + 1)
                for c in range(FC):
                    last = nc.tensor.transpose(ol[:, k, c * P:(c + 1) * P], hid[:, k, c * P:(c + 1) * P], ident)
                last.then_inc(hidT_done, 1)

            def up(s, k, e):
                pe.wait_ge(pgT_kept, s + 1)
                nc.tensor.matmul(sc[:, k, :], pgT[:, k, :], w1_sb[:, bass.ds(e * FF, FF)],
                                 start=True, stop=True).then_inc(up_done, 1)

            def down(s, k, e):
                pe.wait_ge(hidT_kept, s + 1)
                for c in range(FC):
                    last = nc.tensor.matmul(sc[:, 2 + k, 0:D], hidT[:, k, c * P:(c + 1) * P],
                                            w2_sb[:, bass.ds(e * (FC * D) + c * D, D)],
                                            start=(c == 0), stop=(c == FC - 1))
                last.then_inc(down_done, 1)

            transpose_page(0, 0)
            transpose_page(1, 1)
            _, e0, e1, _ = load_experts(pe, 0)
            up(0, 0, e0)
            transpose_page(2, 0)
            transpose_hidden(0, 0)
            up(1, 1, e1)
            down(0, 0, e0)
            with pe.Fori(2, PAGES - 1, 2) as s:
                before_s, of_s, after_s, _ = load_experts(pe, s)
                transpose_page(s + 1, 1)
                transpose_hidden(s - 1, 1)
                up(s, 0, of_s)
                down(s - 1, 1, before_s)
                transpose_page(s + 2, 0)
                transpose_hidden(s, 0)
                up(s + 1, 1, after_s)
                down(s, 0, of_s)
            before_s, of_s, _, _ = load_experts(pe, PAGES - 1)
            transpose_hidden(PAGES - 2, 1)
            up(PAGES - 1, 0, of_s)
            down(PAGES - 2, 1, before_s)
            transpose_hidden(PAGES - 1, 0)
            down(PAGES - 1, 0, of_s)

        @block.vector
        def _(dve):
            V = nc.vector
            steps = [0]

            def link(ins):
                steps[0] += 1
                ins.then_inc(dve_step, 1)
                dve.wait_ge(dve_step, steps[0])

            def stats(b, src, st, mv, signal):
                for t in range(TT):
                    ins = V.bn_stats(st[:, b * TT + t, :], src(t))
                    if t < TT - 1:
                        ins.then_inc(dve_step, 1)
                        steps[0] += 1
                    else:
                        link(ins)
                for t in range(TT):
                    ins = V.bn_aggr(mv[:, b * TT + t, :], st[:, b * TT + t, :])
                    if t < TT - 1:
                        ins.then_inc(dve_step, 1)
                        steps[0] += 1
                    else:
                        ins.then_inc(signal, 1)

            def stats1(b):
                dve.wait_ge(ld_x[b], 16)
                stats(b, lambda t: x_in[:, b * TT + t, :], st1, mv1, ln1_stats)

            def k_low(g):
                dve.wait_ge(k_hi_kept, g + 1)
                for q in (1, 3):
                    r = slice(32 * q, 32 * q + 32)
                    part = k_parts[r, g].rearrange("p b k -> p (b k)")
                    V.scalar_tensor_tensor(part.bitcast(f32r), sc[r, g, 0:BATCH * CTX], bk_rep[r, g:g + 1], part,
                                           ALU.add, ALU.subtract).then_inc(k_kept, 1)

            def keep_values(m, b):
                return V.tensor_tensor(v_blk[:, b], m[:, 0:CHUNKS * D].rearrange("p (m h d) -> p m h d", h=GH, d=DH),
                                       row_mask.unsqueeze(3).to_broadcast([P, CHUNKS * GROUPS, GH, DH]), ALU.mult)

            def q_low(b, g):
                m = mi_wait(dve, "q", b, g)
                dve.wait_ge(q_hi_kept, b * GROUPS + g + 1)
                r = slice(P // 2, P)
                part = q_parts[r, b % 2, g, :]
                V.scalar_tensor_tensor(part, m[r, :], bq_rep[r, g:g + 1], part.bitcast(f32),
                                       ALU.add, ALU.subtract).then_inc(mi_dve, 1)

            def max_tile(b, t):
                if b and t == 0:
                    dve.wait_ge(nmax_split, b)
                for g in range(GROUPS):
                    m = mi_wait(dve, "a", b, t * GROUPS + g)
                    V.tensor_reduce(nmax[:, t, g * GH:(g + 1) * GH], m[:, 0:GK].rearrange("p (h k) -> p h k", k=CTX),
                                    AX.X, ALU.max, negate=True).then_inc(mi_dve, 1)

            def split_max(b):
                dve.wait_ge(mi_dve, read_count(job("a", b, TT * GROUPS - 1)))
                if b:
                    dve.wait_ge(mi_filled, job("mT", b - 1) + 1)
                hi, lo = nmax_parts[:, :, 0:HEADS], nmax_parts[:, :, HEADS:2 * HEADS]
                link(V.tensor_copy(hi, nmax[:, :, :]))
                V.tensor_tensor(lo, nmax[:, :, :], hi.bitcast(f32), ALU.subtract).then_inc(nmax_split, 1)

            def normalise(b):
                dve.wait_ge(sums_done, CHUNKS * (b + 1))
                link(V.reciprocal(rden[:, :], ol[:, 1, :]))
                if b:
                    dve.wait_ge(mi_filled, job("y", b - 1) + 1)
                V.tensor_tensor(attnT[:, :], ol[:, 0, :], rden[:, :], ALU.mult).then_inc(attn_kept, 1)

            def residual(b):
                m = mi_wait(dve, "y", b)
                dve.wait_ge(xb_kept, b + 1)
                t0 = b * TT
                V.tensor_tensor(rows[:, t0:t0 + TT, D:2 * D], m.rearrange("p (t d) -> p t d", d=D), xb[:, b % 2],
                                ALU.add).then_inc(mi_dve, 1)
                dve.wait_ge(mi_dve, read_count(job("y", b)))
                stats(b, lambda t: rows[:, t0 + t, D:2 * D], st2, mv2, ln2_stats)

            def bc(ap):
                return ap.unsqueeze(2).to_broadcast([P, TT, EXPERTS])

            def over_t(ap):
                return ap.unsqueeze(1).to_broadcast([P, TT, EXPERTS])

            def choose(b):
                m = mi_wait(dve, "lg", b)
                if b == 0:
                    dve.wait_ge(ld_ffn, 96)
                    dve.wait_ge(pads_zero, 6)
                else:
                    dve.wait_ge(mi_filled, job("rk", b - 1) + 1)
                V.tensor_tensor(lg[:, :, :], m[:, 0:TT * EXPERTS].rearrange("p (t e) -> p t e", e=EXPERTS),
                                over_t(rb_bc[:, :]), ALU.add).then_inc(mi_dve, 1)
                dve.wait_ge(mi_dve, read_count(job("lg", b)))
                link(V.tensor_reduce(mx[:, :], lg[:, :, :], AX.X, ALU.max))
                V.tensor_tensor(ex[:, :, :], lg[:, :, :], bc(mx[:, :]), ALU.subtract).then_inc(shifted, 1)
                link(V.tensor_tensor(offs[:, :, :], lg[:, :, :], bc(mx[:, :]), ALU.is_ge))
                link(V.tensor_tensor(offs[:, :, :], offs[:, :, :], over_t(rev), ALU.mult))
                link(V.tensor_reduce(mx[:, :], offs[:, :, :], AX.X, ALU.max))
                link(V.tensor_tensor(one_hot[:, :, :], offs[:, :, :], bc(mx[:, :]), ALU.is_equal))
                for t in range(TT):
                    ins = V.tensor_tensor(before[:, t + 1, :], before[:, t, :], one_hot[:, t, :], ALU.add)
                    if t < TT - 1:
                        link(ins)
                    else:
                        ins.then_inc(one_hot_kept, 1)
                dve.wait_ge(ex_kept, b + 1)
                link(V.reduce_sum(den[:, :], ex[:, :, :], AX.X))
                link(V.reciprocal(rows[:, b * TT:(b + 1) * TT, 2 * D], den[:, :]))

            def route(b):
                new, old = (b + 1) % 2, b % 2
                if b == 0:
                    link(V.memset(total[:, old, :], 0.0))
                    link(V.memset(npages[:, old, :], 0.0))
                    link(V.memset(base[:, :], 0.0))
                    link(V.memset(ends[:, 0, :], 0.0))
                    link(V.memset(page_ex[:, :], 0.0))
                used = ends[:, b, EXPERTS - 1:EXPERTS]
                w = TT * EXPERTS
                m = mi_wait(dve, "rk", b)
                link(V.tensor_tensor(total[:, new, :], m[:, w:w + EXPERTS], total[:, old, :], ALU.add))
                V.tensor_tensor(rank[:, :, :], m[:, 0:w].rearrange("p (t e) -> p t e", e=EXPERTS),
                                over_t(total[:, old, :]), ALU.add).then_inc(mi_dve, 1)
                link(V.tensor_tensor(cmp_pg[:, :, :], page_edges.unsqueeze(1).to_broadcast([P, EXPERTS, TILES]),
                                     total[:, new, :].unsqueeze(2).to_broadcast([P, EXPERTS, TILES]), ALU.is_lt))
                link(V.reduce_sum(npages[:, new, :], cmp_pg[:, :, :], AX.X))
                link(V.tensor_tensor(fresh[:, :], npages[:, new, :], npages[:, old, :], ALU.subtract))
                link(V.tensor_tensor_scan(ends[:, b + 1, :], ones[:, 0:EXPERTS], fresh[:, :], used, ALU.mult, ALU.add))
                link(V.tensor_tensor(move[:, :], ends[:, b + 1, :], npages[:, new, :], ALU.subtract))
                link(V.scalar_tensor_tensor(move[:, :], move[:, :], float(P), base[:, :], ALU.mult, ALU.subtract))
                link(V.tensor_scalar(edge[:, :], npages[:, old, :], float(P), None, ALU.mult))
                dve.wait_ge(mi_dve, read_count(job("rk", b)))
                link(V.tensor_tensor(offs[:, :, :], rank[:, :, :], over_t(edge[:, :]), ALU.is_ge))
                link(V.tensor_tensor(offs[:, :, :], offs[:, :, :], over_t(move[:, :]), ALU.mult))
                link(V.tensor_tensor(offs[:, :, :], offs[:, :, :], over_t(base[:, :]), ALU.add))
                link(V.tensor_tensor(offs[:, :, :], offs[:, :, :], rank[:, :, :], ALU.add))
                link(V.tensor_tensor(offs[:, :, :], offs[:, :, :], one_hot[:, :, :], ALU.mult))
                link(V.reduce_sum(mx[:, :], offs[:, :, :], AX.X))
                V.tensor_copy(slot_no[:, b * TT:(b + 1) * TT], mx[:, :]).then_inc(routed, 1)
                link(V.scalar_tensor_tensor(move[:, :], fresh[:, :], 0.0, move[:, :], ALU.is_gt, ALU.mult))
                link(V.tensor_tensor(base[:, :], base[:, :], move[:, :], ALU.add))
                link(V.tensor_tensor(cmp_ex[:, :, :], ends[:, b + 1, :].unsqueeze(1).to_broadcast([P, PAGES, EXPERTS]),
                                     page_no.unsqueeze(2).to_broadcast([P, PAGES, EXPERTS]), ALU.is_le))
                link(V.reduce_sum(owner[:, :], cmp_ex[:, :, :], AX.X))
                link(V.tensor_scalar(owner[:, :], owner[:, :], float(EXPERTS - 1), None, ALU.min))
                link(V.scalar_tensor_tensor(owner[:, :], page_no, used, owner[:, :], ALU.is_ge, ALU.mult))
                link(V.scalar_tensor_tensor(owner[:, :], page_no, ends[:, b + 1, EXPERTS - 1:EXPERTS], owner[:, :],
                                            ALU.is_lt, ALU.mult))
                link(V.tensor_tensor(page_ex[:, 1:PAGES + 1], page_ex[:, 1:PAGES + 1], owner[:, :], ALU.add))

            stats1(0)
            dve.wait_ge(b_kept, 1)
            dve.wait_ge(ld_bias, 64)
            for g in range(GROUPS):
                k_low(g)
            dve.wait_ge(ld_cst, 16)
            dve.wait_ge(k_kept, 2 * GROUPS)
            for g in range(GROUPS):
                V.tensor_tensor(k_blk[:, 0, g, 0:GK].rearrange("p (h k) -> p h k", k=CTX),
                                k_parts[:, g, 0, :].unsqueeze(1).to_broadcast([P, GH, CTX]),
                                head_mask.unsqueeze(2).to_broadcast([P, GH, CTX]), ALU.mult).then_inc(k_blk_kept, 1)
            for b in range(2):
                dve.wait_ge(v_done, b + 1)
                keep_values(ol[:, b, :], b).then_inc(v_kept, 1)
            V.tensor_tensor(bo2[:, :], ol[:, 1, CHUNKS * D:(CHUNKS + 1) * D], bo_bc[:, :], ALU.add).then_inc(bo2_kept, 1)
            for g in range(GROUPS):
                q_low(0, g)
            stats1(1)
            for b in range(2, BATCH):
                keep_values(mi_wait(dve, "v", b), b).then_inc(mi_dve, 1)
            for t in range(TT):
                max_tile(0, t)
            split_max(0)
            for b in range(BATCH):
                n = b + 1
                if b:
                    residual(b - 1)
                if n < BATCH:
                    for g in range(GROUPS):
                        q_low(n, g)
                    max_tile(n, 0)
                if b:
                    choose(b - 1)
                if b + 2 < BATCH:
                    stats1(b + 2)
                if n < BATCH:
                    max_tile(n, 1)
                    max_tile(n, 2)
                normalise(b)
                if n < BATCH:
                    max_tile(n, 3)
                    split_max(n)
                if b:
                    route(b - 1)
            residual(BATCH - 1)
            choose(BATCH - 1)
            route(BATCH - 1)
            V.tensor_copy(page_exi[:, :, 0:2], page_ex[:, 0:2 * STEPS].rearrange("p (i j) -> p i j", j=2)).then_inc(experts_kept, 1)
            V.tensor_copy(page_exi[:, :, 2:4], page_ex[:, 2:2 * STEPS + 2].rearrange("p (i j) -> p i j", j=2)).then_inc(experts_kept, 1)
            dve.wait_ge(experts_kept, 2)

            def keep_page(s, k):
                dve.wait_ge(pgT_done, s + 1)
                V.tensor_copy(pgT[:, k, :], mi[:, k, 0:P]).then_inc(pgT_kept, 1)

            def add_b1(s, k, e):
                dve.wait_ge(up_done, s + 1)
                V.tensor_tensor(hid[:, k, :], sc[:, k, :], b1_bc[:, bass.ds(e * FF, FF)], ALU.add).then_inc(hid_kept, 1)

            def finish(s, k, e):
                dve.wait_ge(down_done, s + 1)
                V.tensor_tensor(y_sb[:, k, :], sc[:, 2 + k, 0:D], b2_bc[:, bass.ds(e * D, D)], ALU.add).then_inc(y_kept, 1)
                if not isinstance(s, int) or s >= 2:
                    dve.wait_ge(written[k], 16 * (s // 2) if isinstance(s, int) else 8 * (s - k))
                rest = pg_rest[:, s, :] if isinstance(s, int) else \
                    pg_rest.rearrange("p s r -> p (s r)")[:, bass.ds(s * REST, REST)]
                V.tensor_copy(gate_tok[:, k, :], rest[:, D:REST]).then_inc(tok_kept, 1)
                dve.wait_ge(y_kept, s + 1)
                dve.wait_ge(tok_kept, s + 1)
                V.scalar_tensor_tensor(out_sb[:, k, :], y_sb[:, k, :], gate_tok[:, k, 0:1], rest[:, 0:D],
                                       ALU.mult, ALU.add).then_inc(out_kept, 1)

            keep_page(0, 0)
            _, e0, e1, _ = load_experts(dve, 0)
            keep_page(1, 1)
            add_b1(0, 0, e0)
            keep_page(2, 0)
            add_b1(1, 1, e1)
            dve.wait_ge(rest_loaded, 16 * len(REST_CUTS))
            finish(0, 0, e0)

            def two_pages(s):
                before_s, of_s, after_s, _ = load_experts(dve, s)
                keep_page(s + 1, 1)
                add_b1(s, 0, of_s)
                finish(s - 1, 1, before_s)
                keep_page(s + 2, 0)
                add_b1(s + 1, 1, after_s)
                finish(s, 0, of_s)

            two_pages(2)
            with dve.Fori(4, PAGES - 1, 2) as s:
                two_pages(s)
            before_s, of_s, _, _ = load_experts(dve, PAGES - 1)
            add_b1(PAGES - 1, 0, of_s)
            finish(PAGES - 2, 1, before_s)
            finish(PAGES - 1, 0, of_s)


def constants():
    import numpy as np
    r = np.arange(P)
    c = np.zeros((P, CC), np.float32)
    c[:, C_ID:C_ID + P] = np.eye(P)
    c[:, C_LT:C_LT + P] = r[:, None] < r[None, :]
    c[:, C_ONE:C_ONE + P] = 1
    c[:, C_HM:C_HM + GH] = (r[:, None] % 32) // DH == np.arange(GH)
    head = (np.arange(CHUNKS)[None, :] * P + r[:, None]) // CTX
    mask = (head[:, :, None] == np.arange(GH)).astype(np.float32)
    c[:, C_MC:C_ON] = np.repeat(mask[:, :, None, :], GROUPS, 2).reshape(P, -1)
    c[:, C_ON:C_REV] = np.repeat(mask, DH, 2).reshape(P, -1)
    c[:, C_REV:C_REV + EXPERTS] = EXPERTS - np.arange(EXPERTS)
    c[:, C_PG:C_PG + TILES] = P * np.arange(TILES)
    c[:, C_SL:C_SL + PAGES] = np.arange(PAGES)
    c[:, C_TOK:C_TOK + TILES] = (P * np.arange(TILES)[None, :] + r[:, None]).astype(np.int32).view(np.float32)
    c[:, C_NH:C_NH + 4] = -0.5
    sel = np.zeros((32, GROUPS, CHUNKS, P), np.float32)
    for g in range(GROUPS):
        for h in range(GH):
            for part in range(2):
                sel[part * HEADS + g * GH + h, g] = mask[:, :, h].T
    return c, sel.reshape(32, GROUPS * CHUNKS, P)


_INS = ['x', 'ctx_1024', 'L0_xattn_Wq', 'L0_xattn_bq', 'L0_xattn_Wk', 'L0_xattn_bk', 'L0_xattn_Wv', 'L0_xattn_bv',
        'L0_xattn_Wo', 'L0_xattn_bo', 'L0_ffn_router_W', 'L0_ffn_router_b', 'L0_ffn_W1', 'L0_ffn_b1', 'L0_ffn_W2',
        'L0_ffn_b2']


def kernel(**inputs):
    import numpy as _np
    import concourse.bacc as _bacc
    from concourse import mybir as _mybir
    from concourse.bass_utils import run_bass_kernel_spmd as _run

    nc = _bacc.Bacc("TRN2", target_bir_lowering=False, num_devices=1)
    cst, sel = constants()
    given = [(n, _np.ascontiguousarray(inputs[n])) for n in _INS] + [("constants", cst), ("selector", sel)]
    arrays, args = {}, []
    for name, a in given:
        arrays[f"in_{name}"] = a
        args.append(nc.dram_tensor(f"in_{name}", a.shape, _mybir.dt.from_np(a.dtype), kind="ExternalInput").ap())
    args.append(nc.dram_tensor("out_0", (BATCH, SEQ, D), _mybir.dt.float32, kind="ExternalOutput").ap())
    layer(nc, *args)
    r = _run(nc, [arrays], core_ids=[0])
    return r.results[0]["out_0"]
```

```python
import concourse.bass as bass
from concourse import mybir
from contextlib import ExitStack

P = 128
BATCH, SEQ, D = 4, 512, 128
CTX = 77
HEADS, DH = 16, 8
GROUPS = 4
GH = HEADS // GROUPS
GK = GH * CTX
CHUNKS = -(-GK // P)
GKP = CHUNKS * P
EXPERTS, FF = 8, 512
FC = FF // P
TT = SEQ // P
TILES = BATCH * TT
ROUNDS = [(0, TILES - TT), (TILES - TT, TILES)]
PAGES = TILES + EXPERTS - 1
STEPS = (PAGES + 1) // 2
ROW = 2 * D + 2
REST = ROW - D
NO_TOKEN = BATCH * SEQ
EPS = 1e-5
SCALE = float(DH) ** -0.5

C_ID, C_LT, C_ONE = 0, P, 2 * P
C_HM = 3 * P
C_MC = C_HM + GH
C_ON = C_MC + CHUNKS * GROUPS * GH
C_REV = C_ON + CHUNKS * 32
C_LO = C_REV + EXPERTS
C_RS = C_LO + 2
C_PG = C_RS + EXPERTS * TILES
C_SL = C_PG + TILES
C_TOK = C_SL + PAGES
C_NH = C_TOK + TILES
CC = C_NH + 4


def layer(nc, x, ctx, Wq, bq, Wk, bk, Wv, bv, Wo, bo, rW, rb, W1, b1, W2, b2, cst, sel, out):
    f32, f32r, i32 = mybir.dt.float32, mybir.dt.float32r, mybir.dt.int32
    ALU, ACT, AX = mybir.AluOpType, mybir.ActivationFunctionType, mybir.AxisListType

    x_v = x.rearrange("b (t p) d -> b p t d", p=P)
    out_rows = out.rearrange("b s d -> (b s) d")
    slots = nc.dram_tensor("slots", [PAGES * P, ROW], f32, kind="Internal").ap()

    with ExitStack() as es:
        def sb(name, shape, dt=f32):
            return es.enter_context(nc.sbuf_tensor(name, shape, dt))

        def sem(name):
            return es.enter_context(nc.semaphore(name))

        cs = sb("cs", [P, CC])
        ident, ltri, ones = cs[:, C_ID:C_ID + P], cs[:, C_LT:C_LT + P], cs[:, C_ONE:C_ONE + P]
        head_mask = cs[:, C_HM:C_HM + GH]
        row_mask = cs[:, C_MC:C_ON].rearrange("p (m h) -> p m h", h=GH)
        ones_mask = cs[:, C_ON:C_REV].rearrange("p (c m) -> p c m", m=32)
        is_low, sign_low = cs[:, C_LO:C_LO + 1], cs[:, C_LO + 1:C_LO + 2]
        rev, page_edges = cs[:, C_REV:C_REV + EXPERTS], cs[:, C_PG:C_PG + TILES]
        page_no, token_no = cs[:, C_SL:C_SL + PAGES], cs[:, C_TOK:C_TOK + TILES]
        neg_half = cs[:, C_NH:C_NH + 4]
        selr = sb("selr", [P, GROUPS * CHUNKS, P], f32r)
        w_in = sb("w_in", [P, 4, D])
        wq_rep, wk_rep = sb("wq_rep", [P, GROUPS, 4, 32]), sb("wk_rep", [P, GROUPS, 4, 32])
        wvT, woT = sb("wvT", [P, D]), sb("woT", [P, D])
        b_in, b_cols = sb("b_in", [2 * GROUPS + 1, D]), sb("b_cols", [P, 2 * GROUPS + 1])
        bq_rep, bk_rep, bv_col = b_cols[:, 0:GROUPS], b_cols[:, GROUPS:2 * GROUPS], b_cols[:, 2 * GROUPS:2 * GROUPS + 1]
        bv_bc = sb("bv_bc", [P, P])
        bo_bc, bo2 = sb("bo_bc", [P, D]), sb("bo2", [P, D])
        rw_sb, rb_bc = sb("rw_sb", [P, EXPERTS]), sb("rb_bc", [P, EXPERTS])
        w1_sb, w2_sb = sb("w1_sb", [P, EXPERTS * FF]), sb("w2_sb", [P, EXPERTS * FC * D])
        b1_bc, b2_bc = sb("b1_bc", [P, EXPERTS * FF]), sb("b2_bc", [P, EXPERTS * D])
        ctx_in = sb("ctx_in", [CTX, BATCH, D])
        ctxT = sb("ctxT", [P, BATCH, 5, CTX])
        k_parts = sb("k_parts", [P, GROUPS, BATCH, CTX])
        bk_low = sb("bk_low", [P, GROUPS])
        k_blk = sb("k_blk", [P, BATCH, GROUPS, GKP], f32r)
        v_blk = sb("v_blk", [P, BATCH, CHUNKS * GROUPS, GH, DH])
        tokens = sb("tokens", [P, (TILES + 2 * TT) * D])
        x_in = tokens[:, 0:TILES * D].rearrange("p (t d) -> p t d", d=D)
        xb = tokens[:, TILES * D:].rearrange("p (b t d) -> p b t d", b=2, d=D)
        pg_rest = tokens[:, 0:PAGES * REST].rearrange("p (s r) -> p s r", r=REST)
        st1, mv1 = sb("st1", [P, TILES, 6]), sb("mv1", [P, TILES, 2])
        st2, mv2 = sb("st2", [P, TILES, 6]), sb("mv2", [P, TILES, 2])
        rstd, shift = sb("rstd", [P, 2, TILES]), sb("shift", [P, 2, TILES])
        xn = sb("xn", [P, 2, TT, D])
        xnT = sb("xnT", [P, SEQ])
        q_parts = sb("q_parts", [P, 2, GROUPS, SEQ], f32r)
        nmax = sb("nmax", [P, TT, HEADS])
        nmax_parts = sb("nmax_parts", [P, TT, 2 * HEADS], f32r)
        nmaxT = sb("nmaxT", [P, 2, SEQ], f32r)
        probs = sb("probs", [P, 2, GROUPS, SEQ])
        den_hd = sb("den_hd", [P, SEQ])
        rden = sb("rden", [P, TT, HEADS])
        rden_t = sb("rden_t", [P, TT, HEADS, DH])
        rden_hd = sb("rden_hd", [P, SEQ])
        attnT = sb("attnT", [P, SEQ])
        rows = sb("rows", [P, TILES, ROW])
        xn2T = sb("xn2T", [P, SEQ])
        lg = sb("lg", [P, EXPERTS, TILES])
        ex, one_hot, upto = (sb(n, [P, EXPERTS * TILES]) for n in ("ex", "one_hot", "upto"))
        top, rank, offs, fresh_part = (sb(n, [P, EXPERTS * TILES]) for n in ("top", "rank", "offs", "fresh_part"))
        mx, den = sb("mx", [P, TILES]), sb("den", [P, TILES])
        total = sb("total", [P, 2, EXPERTS])
        cmp_pg = sb("cmp_pg", [P, EXPERTS, TILES])
        npages = sb("npages", [P, 2, EXPERTS])
        fresh = sb("fresh", [P, EXPERTS])
        ends = sb("ends", [P, len(ROUNDS) + 1, EXPERTS])
        edge, move, base = sb("edge", [P, EXPERTS]), sb("move", [P, EXPERTS]), sb("base", [P, EXPERTS])
        slot_no = sb("slot_no", [P, TILES], i32)
        cmp_ex = sb("cmp_ex", [P, PAGES, EXPERTS])
        owner = sb("owner", [P, PAGES])
        page_ex = sb("page_ex", [P, 2 * STEPS + 2])
        page_exi = sb("page_exi", [P, STEPS, 4], i32)
        empty = sb("empty", [P, ROW])
        pg = sb("pg", [P, 2, D])
        pgT = sb("pgT", [P, 2, P])
        k_cols = GROUPS * BATCH * CTX
        k_hi = q_parts[:, 1].rearrange("p g s -> p (g s)")[:, 0:k_cols].rearrange("p (g b k) -> p g b k", g=GROUPS, b=BATCH)
        k_low_src = probs[:, 0].rearrange("p g s -> p (g s)")[:, 0:k_cols].rearrange("p (g b k) -> p g b k", g=GROUPS, b=BATCH)
        sel_f = probs[0:32, 1].rearrange("p g s -> p (g s)")[:, 0:GROUPS * CHUNKS * P].rearrange("p (m r) -> p m r", r=P)
        hid, hidT = probs[:, 0, 0:2, :], probs[:, 0, 2:4, :]
        y_sb = sb("y_sb", [P, 2, D])
        out_sb = sb("out_sb", [P, 2, D])
        warm_out = sb("warm_out", [P, 1])
        read_mark = sb("read_mark", [P, 1])
        gate_tok = sb("gate_tok", [P, 2, 2])

        def pb(name, banks):
            return es.enter_context(nc.psum_tensor(name, [P, banks, 512], f32))
        sc = pb("sc", 3)
        mi = pb("mi", 3)
        ol = pb("ol", 2)

        ld_cst, ld_w, ld_ctx, ld_bias, ld_sel = (sem(n) for n in ("ld_cst", "ld_w", "ld_ctx", "ld_bias", "ld_sel"))
        ld_x = [sem(f"ld_x{b}") for b in range(BATCH)]
        ld_ffn = sem("ld_ffn")
        slots_empty = sem("slots_empty")
        wT_done, ctxT_done, w_kept, ctx_kept = sem("wT_done"), sem("ctxT_done"), sem("w_kept"), sem("ctx_kept")
        k_done, k_hi_kept, k_kept, k_blk_kept = sem("k_done"), sem("k_hi_kept"), sem("k_kept"), sem("k_blk_kept")
        den_kept, rden_kept, rden_t_kept, warm = sem("den_kept"), sem("rden_kept"), sem("rden_t_kept"), sem("warm")
        selr_zero, bk_low_kept, ld_wvo = sem("selr_zero"), sem("bk_low_kept"), sem("ld_wvo")
        bo2_kept = sem("bo2_kept")
        pads_zero, sel_kept, bv_kept = sem("pads_zero"), sem("sel_kept"), sem("bv_kept")
        b_kept = sem("b_kept")
        ln1_stats, xn_kept, xb_kept = sem("ln1_stats"), sem("xn_kept"), sem("xb_kept")
        ln2_stats, xn2_kept = sem("ln2_stats"), sem("xn2_kept")
        mi_filled = sem("mi_filled")
        mi_act = sem("mi_act")
        mi_dve = sem("mi_dve")
        q_hi_kept = sem("q_hi_kept")
        nmax_split = sem("nmax_split")
        sc_filled, exp_done = sem("sc_filled"), sem("exp_done")
        sums_done = sem("sums_done")
        attn_kept, scatters = sem("attn_kept"), sem("scatters")
        shifted, ex_kept = sem("shifted"), sem("ex_kept")
        one_hot_kept = sem("one_hot_kept")
        routed, sent = sem("routed"), sem("sent")
        experts_kept = sem("experts_kept")
        pool_step, dve_step = sem("pool_step"), sem("dve_step")
        rest_loaded = sem("rest_loaded")
        pg_loaded = [sem("pg_loaded0"), sem("pg_loaded1")]
        pgT_done, pgT_kept = sem("pgT_done"), sem("pgT_kept")
        up_done, hid_kept = sem("up_done"), sem("hid_kept")
        hidT_done, hidT_kept = sem("hidT_done"), sem("hidT_kept")
        down_done, y_kept, out_kept = sem("down_done"), sem("y_kept"), sem("out_kept")
        tok_kept = sem("tok_kept")
        written = [sem("written0"), sem("written1")]

        REST_CUTS = [(0, 2), (2, 8), (8, PAGES)]

        JOBS = [("w", 0, 0), ("c", 0, 0), ("xT", 0, 0), ("w", 1, 0)]
        JOBS += [("q", 0, g) for g in range(GROUPS)]
        for g in range(GROUPS):
            JOBS += [("a", 0, g * TT + t) for t in range(TT)] + [("v", g, 0)]
        JOBS += [("mT", 0, 0)]
        for b in range(BATCH):
            n = b + 1
            more = n < BATCH
            if more:
                JOBS += [("xT", n, 0)]
            if b:
                JOBS += [("rT", b - 1, 0)]
            if more:
                JOBS += [("q", n, 0)]
            if b:
                JOBS += [("y", b - 1, 0)]
            if more:
                JOBS += [("q", n, 1)] + [("a", n, t) for t in range(TT)] + [("q", n, 2)]
                JOBS += [("a", n, TT + t) for t in range(TT)] + [("q", n, 3)]
                JOBS += [("a", n, 2 * TT + t) for t in range(TT)]
            if b:
                JOBS += [("x2T", b - 1, 0)]
            if more:
                JOBS += [("a", n, 3 * TT + t) for t in range(TT)]
            if b:
                JOBS += [("lg", b - 1, 0)]
            if more:
                JOBS += [("mT", n, 0)]
            JOBS += [("dT", b, 0)]
        JOBS += [("rT", BATCH - 1, 0), ("y", BATCH - 1, 0), ("rk", 0, 0), ("x2T", BATCH - 1, 0), ("lg", BATCH - 1, 0), ("rk", 1, 0)]
        BY_ACT = ("w", "c", "xT", "mT", "x2T", "rT")

        def read_count(i):
            act = JOBS[i][0] in BY_ACT
            return sum((j[0] in BY_ACT) == act for j in JOBS[:i + 1])

        def job(kind, b=0, i=0):
            return JOBS.index((kind, b, i))

        def load_experts(eng, s):
            row = page_exi[0:1, s // 2, :] if isinstance(s, int) else \
                page_exi[0:1].rearrange("p i j -> p (i j)")[:, bass.ds(s * 2, 4)]
            return nc.values_load_multi_w_load_instructions(
                row, engines=(eng.engine,), min_val=0, max_val=EXPERTS - 1,
                skip_runtime_bounds_check_because="the table is clamped to the experts' numbers")[1]

        def mi_take(pe, kind, b=0, i=0):
            n = job(kind, b, i)
            if n >= 3:
                pe.wait_ge(mi_act if JOBS[n - 3][0] in BY_ACT else mi_dve, read_count(n - 3))
            return mi[:, n % 3]

        def mi_wait(eng, kind, b=0, i=0):
            n = job(kind, b, i)
            eng.wait_ge(mi_filled, n + 1)
            return mi[:, n % 3]

        block = es.enter_context(nc.Block())

        @block.sync
        def _(sp):
            sp.dma_start(cs[:, :], cst).then_inc(ld_cst, 16)
            for i, w in enumerate((Wq, Wk)):
                sp.dma_start(w_in[:, i, :], w).then_inc(ld_w, 16)
            for i, w in enumerate((Wv, Wo)):
                sp.dma_start(w_in[:, 2 + i, :], w).then_inc(ld_wvo, 16)
            for b in range(1, BATCH):
                sp.dma_start(x_in[:, b * TT:(b + 1) * TT, :], x_v[b]).then_inc(ld_x[b], 16)
            sp.dma_start(rw_sb[:, :], rW).then_inc(ld_ffn, 16)
            sp.dma_start(rb_bc[:, :], rb.unsqueeze(0).to_broadcast([P, EXPERTS])).then_inc(ld_ffn, 16)
            sp.wait_ge(pads_zero, 2)
            sp.dma_start(slots.rearrange("(s p) r -> p s r", p=P),
                         empty[:, :].unsqueeze(1).to_broadcast([P, PAGES, ROW])).then_inc(slots_empty, 16)
            sp.dma_start(w1_sb[:, :].rearrange("p (e f) -> p e f", e=EXPERTS),
                         W1.rearrange("e d f -> d e f")).then_inc(ld_ffn, 16)
            sp.dma_start(w2_sb[:, :].rearrange("p (e d) -> p e d", d=D),
                         W2.rearrange("e (c p) d -> p (e c) d", p=P)).then_inc(ld_ffn, 16)
            sp.dma_start(b1_bc[:, :], b1.rearrange("e f -> (e f)").unsqueeze(0).to_broadcast([P, EXPERTS * FF])).then_inc(ld_ffn, 16)
            sp.dma_start(b2_bc[:, :], b2.rearrange("e d -> (e d)").unsqueeze(0).to_broadcast([P, EXPERTS * D])).then_inc(ld_ffn, 16)

            sp.wait_ge(sent, 16 * TILES)
            slots_v = slots.rearrange("(s p) r -> s p r", p=P)
            for k in range(2):
                sp.dma_start(pg[:, k, :], slots_v[k, :, 0:D]).then_inc(pg_loaded[k], 16)
            for i, (s0, s1) in enumerate(REST_CUTS):
                sp.dma_start(pg_rest[:, s0:s1, :], slots_v[s0:s1, :, D:ROW].rearrange("s p r -> p s r")).then_inc(rest_loaded, 16)

            def load(s, k):
                sp.wait_ge(pgT_done, s + 1)
                sp.dma_start(pg[:, k, :], slots_v[bass.ds(s + 2, 1), :, 0:D].rearrange("s p r -> (s p) r")).then_inc(pg_loaded[k], 16)

            with sp.Fori(0, PAGES - 3, 2) as s:
                load(s, 0)
                load(s + 1, 1)
            load(PAGES - 3, 0)

        @block.gpsimd
        def _(pool):
            steps = [0]

            def link(ins):
                steps[0] += 1
                ins.then_inc(pool_step, 1)
                pool.wait_ge(pool_step, steps[0])

            nc.gpsimd.memset(empty[:, 0:ROW - 1], 0.0).then_inc(pads_zero, 1)
            nc.gpsimd.memset(empty[:, ROW - 1:ROW].bitcast(i32), NO_TOKEN).then_inc(pads_zero, 1)
            nc.gpsimd.memset(k_blk[:, :, :, GK:GKP].bitcast(f32), 0.0).then_inc(pads_zero, 1)

            def norm(which, mv, b, src, dst, signal):
                t0 = b * TT
                r, s = rstd[:, which, t0:t0 + TT], shift[:, which, t0:t0 + TT]
                link(nc.gpsimd.tensor_scalar(s, mv[:, t0:t0 + TT, 1], EPS, 1.0, ALU.add, ALU.mult))
                link(nc.gpsimd.tensor_tensor(r, s, neg_half, ALU.pow))
                link(nc.gpsimd.tensor_tensor(s, mv[:, t0:t0 + TT, 0], r, ALU.mult))
                link(nc.gpsimd.tensor_scalar(s, s, -1.0, 0.0, ALU.mult, ALU.add))
                for t in range(TT):
                    nc.gpsimd.tensor_scalar(dst(t), src(t), rstd[:, which, t0 + t:t0 + t + 1],
                                            shift[:, which, t0 + t:t0 + t + 1], ALU.mult, ALU.add).then_inc(signal, 1)

            def ln1(b):
                pool.wait_ge(ln1_stats, b + 1)
                if b == 0:
                    pool.wait_ge(ld_cst, 16)
                if b >= 2:
                    pool.wait_ge(mi_filled, job("xT", b - 2) + 1)
                norm(0, mv1, b, lambda t: x_in[:, b * TT + t, :], lambda t: xn[:, b % 2, t, :], xn_kept)

            def x_plus_bias(b):
                pool.wait_ge(bo2_kept, 1)
                if b >= 2:
                    pool.wait_ge(mi_dve, read_count(job("y", b - 2)))
                nc.gpsimd.tensor_tensor(xb[:, b % 2], x_in[:, b * TT:(b + 1) * TT, :],
                                        bo2[:, :].unsqueeze(1).to_broadcast([P, TT, D]), ALU.add).then_inc(xb_kept, 1)

            def k_block(b):
                if b == 1:
                    pool.wait_ge(k_kept, 1)
                for g in range(GROUPS):
                    nc.gpsimd.tensor_tensor(k_blk[:, b, g, 0:GK].rearrange("p (h k) -> p h k", k=CTX),
                                            k_parts[:, g, b, :].unsqueeze(1).to_broadcast([P, GH, CTX]),
                                            head_mask.unsqueeze(2).to_broadcast([P, GH, CTX]),
                                            ALU.mult).then_inc(k_blk_kept, 1)

            def send(r):
                if r == 0:
                    pool.wait_ge(slots_empty, 16)
                    pool.wait_ge(sel_kept, 2)
                pool.wait_ge(routed, r + 1)
                for t in range(*ROUNDS[r]):
                    pool.indirect_dma_start(slots, bass.IndirectOffsetOnAxis(ap=slot_no[:, t:t + 1], axis=0),
                                            rows[:, t, :], None).then_inc(sent, 16)

            ln1(0)
            pool.wait_ge(selr_zero, 1)
            pool.wait_ge(ld_sel, 16)
            nc.gpsimd.tensor_copy(selr[0:32, :, :], sel_f[:, :, :]).then_inc(sel_kept, 1)
            nc.gpsimd.tensor_copy(rows[:, :, ROW - 1].bitcast(i32), token_no.bitcast(i32)).then_inc(sel_kept, 1)
            k_block(1)
            ln1(1)
            x_plus_bias(0)
            x_plus_bias(1)
            for b in range(BATCH):
                if b >= 1:
                    pool.wait_ge(ln2_stats, b)
                    norm(1, mv2, b - 1, lambda t: rows[:, (b - 1) * TT + t, D:2 * D],
                         lambda t: rows[:, (b - 1) * TT + t, 0:D], xn2_kept)
                if b + 2 < BATCH:
                    k_block(b + 2)
                    ln1(b + 2)
                    x_plus_bias(b + 2)
            pool.wait_ge(ln2_stats, BATCH)
            norm(1, mv2, BATCH - 1, lambda t: rows[:, (BATCH - 1) * TT + t, D:2 * D],
                 lambda t: rows[:, (BATCH - 1) * TT + t, 0:D], xn2_kept)
            send(0)
            send(1)

            last_token = pool.to_reg(NO_TOKEN - 1)

            def scatter(s, k):
                pool.wait_ge(out_kept, s + 1)
                pool.sem_inc(scatters, 1)
                pool.indirect_dma_start(out_rows, bass.IndirectOffsetOnAxis(ap=gate_tok[:, k, 1:2].bitcast(i32), axis=0),
                                        out_sb[:, k, :], None, bounds_check=last_token,
                                        oob_is_err=False).then_inc(written[k], 16)

            with pool.Fori(0, PAGES - 1, 2) as s:
                scatter(s, 0)
                scatter(s + 1, 1)
            scatter(PAGES - 1, 0)
            pool.wait_ge(written[0], 16 * ((PAGES + 1) // 2))
            pool.wait_ge(written[1], 16 * (PAGES // 2))

        @block.scalar
        def _(act):
            act.dma_start(x_in[:, 0:TT, :], x_v[0]).then_inc(ld_x[0], 16)
            act.dma_start(ctx_in[:, :, :], ctx.rearrange("b k d -> k b d")).then_inc(ld_ctx, 16)
            act.dma_start(sel_f[:, :, :], sel).then_inc(ld_sel, 16)
            for i, bias in enumerate((bq, bk)):
                act.dma_start(b_in[i * GROUPS:(i + 1) * GROUPS, :].rearrange("g (c r) -> g c r", r=32),
                              bias.rearrange("(g r) -> g r", r=32).unsqueeze(1).to_broadcast([GROUPS, 4, 32])).then_inc(ld_bias, 16)
            act.dma_start(b_in[2 * GROUPS:2 * GROUPS + 1, :], bv.unsqueeze(0)).then_inc(ld_bias, 16)
            act.dma_start(bo_bc[:, :], bo.unsqueeze(0).to_broadcast([P, D])).then_inc(ld_bias, 16)

            act.wait_ge(pads_zero, 1)
            nc.scalar.activation(warm_out[:, :], empty[:, 0:1], ACT.Exp).then_inc(warm, 1)

            m = mi_wait(act, "w", 0)
            nc.scalar.activation(wk_rep[:, :, :, :], m[:, D:2 * D].rearrange("p (g r) -> p g r", r=32)
                                 .unsqueeze(2).to_broadcast([P, GROUPS, 4, 32]), ACT.Copy).then_inc(w_kept, 1)
            nc.scalar.activation(wq_rep[:, :, :, :], m[:, 0:D].rearrange("p (g r) -> p g r", r=32)
                                 .unsqueeze(2).to_broadcast([P, GROUPS, 4, 32]), ACT.Copy).then_inc(mi_act, 1)
            m = mi_wait(act, "c")
            nc.scalar.activation(b_cols[:, :], m[:, BATCH * CTX:BATCH * CTX + 2 * GROUPS + 1], ACT.Copy).then_inc(b_kept, 1)
            nc.scalar.activation(ctxT[:, :, :, :], m[:, 0:BATCH * CTX].rearrange("p (b k) -> p b k", k=CTX)
                                 .unsqueeze(2).to_broadcast([P, BATCH, 5, CTX]), ACT.Copy).then_inc(mi_act, 1)

            def k_sources(g):
                act.wait_ge(k_done, g + 1)
                if g == 0:
                    act.wait_ge(b_kept, 1)
                    act.wait_ge(bk_low_kept, 1)
                m = (sc[:, g] if g < 3 else ol[:, 0])[:, 0:BATCH * CTX]
                nc.scalar.activation(k_hi[:, g].rearrange("p b k -> p (b k)"), m, ACT.Identity,
                                     bias=bk_rep[:, g:g + 1]).then_inc(k_hi_kept, 1)
                nc.scalar.activation(k_low_src[:, g].rearrange("p b k -> p (b k)"), m, ACT.Identity,
                                     bias=bk_low[:, g:g + 1], scale=is_low).then_inc(k_hi_kept, 1)

            def keep_wvo():
                m = mi_wait(act, "w", 1)
                nc.scalar.activation(wvT[:, :], m[:, 0:D], ACT.Copy).then_inc(w_kept, 1)
                nc.scalar.activation(woT[:, :], m[:, D:2 * D], ACT.Copy).then_inc(mi_act, 1)
                nc.scalar.activation(bv_bc[:, :], bv_col.to_broadcast([P, P]), ACT.Copy).then_inc(bv_kept, 1)

            def keep_xT(b):
                m = mi_wait(act, "xT", b)
                if b:
                    act.wait_ge(mi_filled, job("q", b - 1, GROUPS - 1) + 1)
                nc.scalar.activation(xnT[:, :], m, ACT.Copy).then_inc(mi_act, 1)

            def q_hi(b, g):
                m = mi_wait(act, "q", b, g)
                if b >= 2:
                    act.wait_ge(sc_filled, GROUPS * CHUNKS * (b - 1))
                nc.scalar.activation(q_parts[:, b % 2, g, :], m, ACT.Identity,
                                     bias=bq_rep[:, g:g + 1]).then_inc(q_hi_kept, 1)

            def keep_maxT(b):
                if b == 0:
                    act.wait_ge(selr_zero, 2)
                m = mi_wait(act, "mT", b)
                if b >= 2:
                    act.wait_ge(sc_filled, GROUPS * CHUNKS * (b - 1))
                nc.scalar.activation(nmaxT[0:2 * HEADS, b % 2, :], m[0:2 * HEADS, :], ACT.Copy).then_inc(mi_act, 1)

            def exps(b, c, groups=range(GROUPS)):
                n = b * CHUNKS + c
                if n >= 2 and groups[0] == 0:
                    act.wait_ge(sums_done, n - 1)
                for g in groups:
                    j = n * GROUPS + g
                    act.wait_ge(sc_filled, j + 1)
                    nc.scalar.activation(probs[:, n % 2, g, :], sc[:, j % 3, :], ACT.Exp,
                                         scale=SCALE).then_inc(exp_done, 1)

            def keep_den(b):
                act.wait_ge(sums_done, CHUNKS * (b + 1))
                nc.scalar.activation(den_hd[:, :], ol[:, 1, :], ACT.Copy).then_inc(den_kept, 1)

            def spread_rden(b):
                act.wait_ge(rden_kept, b + 1)
                nc.scalar.activation(rden_t[:, :, :, :], rden[:, :, :].unsqueeze(3).to_broadcast([P, TT, HEADS, DH]),
                                     ACT.Copy).then_inc(rden_t_kept, 1)

            def keep_rdenT(b):
                m = mi_wait(act, "rT", b)
                if b:
                    act.wait_ge(attn_kept, b)
                nc.scalar.activation(rden_hd[:, :], m, ACT.Copy).then_inc(mi_act, 1)

            def keep_x2T(b):
                m = mi_wait(act, "x2T", b)
                if b:
                    act.wait_ge(mi_filled, job("lg", b - 1) + 1)
                nc.scalar.activation(xn2T[:, :], m, ACT.Copy).then_inc(mi_act, 1)

            def gate_exp(r):
                act.wait_ge(shifted, r + 1)
                e = ex[:, 0:EXPERTS * (ROUNDS[r][1] - ROUNDS[r][0])]
                nc.scalar.activation(e, e, ACT.Exp).then_inc(ex_kept, 1)

            for g in range(GROUPS):
                k_sources(g)
            keep_xT(0)
            keep_wvo()
            for g in range(GROUPS):
                q_hi(0, g)
            keep_maxT(0)
            for b in range(BATCH):
                n = b + 1
                more = n < BATCH
                exps(b, 0)
                if more:
                    keep_xT(n)
                if b:
                    keep_rdenT(b - 1)
                exps(b, 1, (0, 1))
                if more:
                    q_hi(n, 0)
                exps(b, 1, (2, 3))
                if more:
                    q_hi(n, 1)
                    q_hi(n, 2)
                exps(b, 2, (0, 1))
                if more:
                    q_hi(n, 3)
                exps(b, 2, (2, 3))
                if b:
                    keep_x2T(b - 1)
                keep_den(b)
                if more:
                    keep_maxT(n)
                spread_rden(b)
            gate_exp(0)
            keep_rdenT(BATCH - 1)
            keep_x2T(BATCH - 1)
            gate_exp(1)

            def relu(s, k):
                act.wait_ge(hidT_done, s + 1)
                nc.scalar.activation(hidT[:, k, :], ol[:, k, :], ACT.Relu).then_inc(hidT_kept, 1)

            relu(0, 0)
            with act.Fori(1, PAGES - 1, 2) as s:
                relu(s, 1)
                relu(s + 1, 0)

        @block.tensor
        def _(pe):
            def transpose_weights(i, loaded):
                pe.wait_ge(loaded, 32)
                m = mi_take(pe, "w", i)
                nc.tensor.transpose(m[:, 0:D], w_in[:, 2 * i, :], ident)
                nc.tensor.transpose(m[:, D:2 * D], w_in[:, 2 * i + 1, :], ident).then_inc(mi_filled, 1)

            pe.wait_ge(ld_cst, 16)
            transpose_weights(0, ld_w)
            pe.wait_ge(ld_ctx, 16)
            m = mi_take(pe, "c")
            pe.wait_ge(ld_bias, 64)
            nc.tensor.transpose(m[:, BATCH * CTX:BATCH * CTX + 2 * GROUPS + 1], b_in[:, :],
                                ident[0:2 * GROUPS + 1, 0:2 * GROUPS + 1])
            for b in range(BATCH):
                last = nc.tensor.transpose(m[:, b * CTX:(b + 1) * CTX], ctx_in[:, b, :], ident[0:CTX, 0:CTX])
            last.then_inc(mi_filled, 1)

            def transpose_x(b):
                pe.wait_ge(xn_kept, TT * (b + 1))
                m = mi_take(pe, "xT", b)
                for t in range(TT):
                    last = nc.tensor.transpose(m[:, t * P:(t + 1) * P], xn[:, b % 2, t, :], ident)
                last.then_inc(mi_filled, 1)

            def project_q(b, g):
                if g == 0:
                    pe.wait_ge(mi_act, read_count(job("xT", b)))
                m = mi_take(pe, "q", b, g)
                nc.tensor.matmul(m, wq_rep[:, g].rearrange("p c r -> p (c r)"), xnT[:, :],
                                 start=True, stop=True).then_inc(mi_filled, 1)

            def scores_for_max(b, g):
                pe.wait_ge(mi_dve, read_count(job("q", b, g)))
                if g == 0:
                    pe.wait_ge(k_blk_kept, GROUPS * (b + 1))
                for t in range(TT):
                    m = mi_take(pe, "a", b, g * TT + t)
                    nc.tensor.matmul(m[:, 0:GK], q_parts[:, b % 2, g, t * P:(t + 1) * P], k_blk[:, b, g, 0:GK],
                                     start=True, stop=True).then_inc(mi_filled, 1)

            def transpose_max(b):
                pe.wait_ge(nmax_split, b + 1)
                m = mi_take(pe, "mT", b)
                for t in range(TT):
                    last = nc.tensor.transpose(m[0:2 * HEADS, t * P:(t + 1) * P], nmax_parts[:, t, :].bitcast(f32), ident)
                last.then_inc(mi_filled, 1)

            def scores(b, c, groups=range(GROUPS)):
                if c == 0:
                    pe.wait_ge(mi_act, read_count(job("mT", b)))
                    if b == 0:
                        pe.wait_ge(sel_kept, 1)
                        pe.wait_ge(pads_zero, 3)
                for g in groups:
                    j = (b * CHUNKS + c) * GROUPS + g
                    if j >= 3:
                        pe.wait_ge(exp_done, j - 2)
                    elif j == 0:
                        pe.wait_ge(k_hi_kept, 2 * GROUPS)
                    nc.tensor.matmul(sc[:, j % 3, :], k_blk[:, b, g, c * P:(c + 1) * P], q_parts[:, b % 2, g, :],
                                     start=True, stop=False)
                    nc.tensor.matmul(sc[:, j % 3, :], selr[:, g * CHUNKS + c, :], nmaxT[:, b % 2, :],
                                     start=False, stop=True).then_inc(sc_filled, 1)

            def weighted_sums(b, c):
                n = b * CHUNKS + c
                pe.wait_ge(exp_done, GROUPS * (n + 1))
                if n == 0:
                    pe.wait_ge(mi_dve, read_count(job("v", BATCH - 1)))
                if c == 0 and b:
                    pe.wait_ge(attn_kept, b)
                for g in range(GROUPS):
                    r = slice(32 * g, 32 * g + 32)
                    nc.tensor.matmul(ol[r, 0, :], v_blk[:, b, c * GROUPS + g].rearrange("p h d -> p (h d)"),
                                     probs[:, n % 2, g, :], start=(c == 0), stop=(c == CHUNKS - 1))
                for g in range(GROUPS):
                    r = slice(32 * g, 32 * g + 32)
                    last = nc.tensor.matmul(ol[r, 1, :], ones_mask[:, c, :], probs[:, n % 2, g, :],
                                            start=(c == 0), stop=(c == CHUNKS - 1))
                last.then_inc(sums_done, 1)

            def project_out(b):
                pe.wait_ge(attn_kept, b + 1)
                m = mi_take(pe, "y", b)
                for t in range(TT):
                    last = nc.tensor.matmul(m[:, t * D:(t + 1) * D], attnT[:, t * P:(t + 1) * P], woT[:, :],
                                            start=True, stop=True)
                last.then_inc(mi_filled, 1)

            def transpose_x2(b):
                pe.wait_ge(xn2_kept, TT * (b + 1))
                m = mi_take(pe, "x2T", b)
                for t in range(TT):
                    last = nc.tensor.transpose(m[:, t * P:(t + 1) * P], rows[:, b * TT + t, 0:D], ident)
                last.then_inc(mi_filled, 1)

            def logits(b):
                pe.wait_ge(mi_act, read_count(job("x2T", b)))
                if b == 0:
                    pe.wait_ge(ld_ffn, 96)
                m = mi_take(pe, "lg", b)
                for t in range(TT):
                    last = nc.tensor.matmul(m[:, t * EXPERTS:(t + 1) * EXPERTS], xn2T[:, t * P:(t + 1) * P], rw_sb[:, :],
                                            start=True, stop=True)
                last.then_inc(mi_filled, 1)

            def ranks(r):
                pe.wait_ge(one_hot_kept, r + 1)
                m = mi_take(pe, "rk", r)
                tiles = ROUNDS[r][1] - ROUNDS[r][0]
                w = EXPERTS * tiles
                nc.tensor.matmul(m[:, 0:w], ltri, one_hot[:, 0:w], start=True, stop=False)
                nc.tensor.matmul(m[:, 0:w], ones, upto[:, 0:w], start=False, stop=True)
                nc.tensor.matmul(m[:, w:w + EXPERTS], ones, upto[:, 0:w].rearrange("p (e t) -> p e t", t=tiles)[:, :, tiles - 1],
                                 start=True, stop=True).then_inc(mi_filled, 1)

            def transpose_den(b):
                pe.wait_ge(den_kept, b + 1)
                m = mi_take(pe, "dT", b)
                for t in range(TT):
                    last = nc.tensor.transpose(m[:, t * P:(t + 1) * P], den_hd[:, t * P:(t + 1) * P], ident)
                last.then_inc(mi_filled, 1)

            def transpose_rden(b):
                pe.wait_ge(rden_t_kept, b + 1)
                m = mi_take(pe, "rT", b)
                for t in range(TT):
                    last = nc.tensor.transpose(m[:, t * P:(t + 1) * P], rden_t[:, t].rearrange("p h d -> p (h d)"), ident)
                last.then_inc(mi_filled, 1)

            def values(b):
                m = mi_take(pe, "v", b)
                for c in range(CHUNKS):
                    last = nc.tensor.matmul(m[:, c * D:(c + 1) * D],
                                            ctxT[:, b].rearrange("p r k -> p (r k)")[:, c * P:(c + 1) * P],
                                            wvT[:, :], start=True, stop=True)
                if b == 0:
                    pe.wait_ge(bv_kept, 1)
                    last = nc.tensor.matmul(m[:, CHUNKS * D:(CHUNKS + 1) * D], bv_bc[:, :], woT[:, :],
                                            start=True, stop=True)
                last.then_inc(mi_filled, 1)

            pe.wait_ge(w_kept, 1)
            pe.wait_ge(mi_act, 2)
            for g in range(GROUPS):
                nc.tensor.matmul((sc[:, g] if g < 3 else ol[:, 0])[:, 0:BATCH * CTX],
                                 wk_rep[:, g].rearrange("p c r -> p (c r)"),
                                 ctxT[:, :, 0, :], start=True, stop=True).then_inc(k_done, 1)
            transpose_x(0)
            transpose_weights(1, ld_wvo)
            for g in range(GROUPS):
                project_q(0, g)
            for g in range(GROUPS):
                scores_for_max(0, g)
                if g == 0:
                    pe.wait_ge(w_kept, 2)
                    pe.wait_ge(mi_act, read_count(job("w", 1)))
                values(g)
            transpose_max(0)
            for b in range(BATCH):
                n = b + 1
                more = n < BATCH
                scores(b, 0)
                if more:
                    transpose_x(n)
                if b:
                    transpose_rden(b - 1)
                scores(b, 1, (0, 1))
                if more:
                    project_q(n, 0)
                if b:
                    project_out(b - 1)
                scores(b, 1, (2, 3))
                if more:
                    project_q(n, 1)
                weighted_sums(b, 0)
                if more:
                    scores_for_max(n, 0)
                    project_q(n, 2)
                scores(b, 2, (0, 1))
                if more:
                    scores_for_max(n, 1)
                    project_q(n, 3)
                scores(b, 2, (2, 3))
                if more:
                    scores_for_max(n, 2)
                weighted_sums(b, 1)
                if b:
                    transpose_x2(b - 1)
                if more:
                    scores_for_max(n, 3)
                if b:
                    logits(b - 1)
                weighted_sums(b, 2)
                if more:
                    transpose_max(n)
                transpose_den(b)
            transpose_rden(BATCH - 1)
            project_out(BATCH - 1)
            ranks(0)
            transpose_x2(BATCH - 1)
            logits(BATCH - 1)
            ranks(1)

            pe.wait_ge(ld_ffn, 96)
            pe.wait_ge(experts_kept, 2)

            def transpose_page(s, k):
                pe.wait_ge(pg_loaded[k], 16 * (s // 2 + 1) if isinstance(s, int) else 8 * (s + 2 - k))
                nc.tensor.transpose(mi[:, k, 0:P], pg[:, k, :], ident).then_inc(pgT_done, 1)

            def transpose_hidden(s, k):
                pe.wait_ge(hid_kept, s + 1)
                for c in range(FC):
                    last = nc.tensor.transpose(ol[:, k, c * P:(c + 1) * P], hid[:, k, c * P:(c + 1) * P], ident)
                last.then_inc(hidT_done, 1)

            def up(s, k, e):
                pe.wait_ge(pgT_kept, s + 1)
                nc.tensor.matmul(sc[:, k, :], pgT[:, k, :], w1_sb[:, bass.ds(e * FF, FF)],
                                 start=True, stop=True).then_inc(up_done, 1)

            def down(s, k, e):
                pe.wait_ge(hidT_kept, s + 1)
                for c in range(FC):
                    last = nc.tensor.matmul((sc[:, 2] if k else mi[:, 2])[:, 0:D], hidT[:, k, c * P:(c + 1) * P],
                                            w2_sb[:, bass.ds(e * (FC * D) + c * D, D)],
                                            start=(c == 0), stop=(c == FC - 1))
                last.then_inc(down_done, 1)

            transpose_page(0, 0)
            transpose_page(1, 1)
            _, e0, e1, _ = load_experts(pe, 0)
            up(0, 0, e0)
            transpose_page(2, 0)
            transpose_hidden(0, 0)
            up(1, 1, e1)
            down(0, 0, e0)
            with pe.Fori(2, PAGES - 1, 2) as s:
                before_s, of_s, after_s, _ = load_experts(pe, s)
                transpose_page(s + 1, 1)
                transpose_hidden(s - 1, 1)
                up(s, 0, of_s)
                down(s - 1, 1, before_s)
                transpose_page(s + 2, 0)
                transpose_hidden(s, 0)
                up(s + 1, 1, after_s)
                down(s, 0, of_s)
            before_s, of_s, _, _ = load_experts(pe, PAGES - 1)
            transpose_hidden(PAGES - 2, 1)
            up(PAGES - 1, 0, of_s)
            down(PAGES - 2, 1, before_s)
            transpose_hidden(PAGES - 1, 0)
            down(PAGES - 1, 0, of_s)

        @block.vector
        def _(dve):
            V = nc.vector
            steps = [0]

            def link(ins):
                steps[0] += 1
                ins.then_inc(dve_step, 1)
                dve.wait_ge(dve_step, steps[0])

            def stats(b, src, st, mv, signal):
                for t in range(TT):
                    ins = V.bn_stats(st[:, b * TT + t, :], src(t))
                    if t < TT - 1:
                        ins.then_inc(dve_step, 1)
                        steps[0] += 1
                    else:
                        link(ins)
                for t in range(TT):
                    ins = V.bn_aggr(mv[:, b * TT + t, :], st[:, b * TT + t, :])
                    if t < TT - 1:
                        ins.then_inc(dve_step, 1)
                        steps[0] += 1
                    else:
                        ins.then_inc(signal, 1)

            def stats1(b):
                dve.wait_ge(ld_x[b], 16)
                stats(b, lambda t: x_in[:, b * TT + t, :], st1, mv1, ln1_stats)

            def keep_values(m, b):
                return V.tensor_tensor(v_blk[:, b], m[:, 0:CHUNKS * D].rearrange("p (m h d) -> p m h d", h=GH, d=DH),
                                       row_mask.unsqueeze(3).to_broadcast([P, CHUNKS * GROUPS, GH, DH]), ALU.mult)

            def q_low(b, g):
                m = mi_wait(dve, "q", b, g)
                dve.wait_ge(q_hi_kept, b * GROUPS + g + 1)
                r = slice(P // 2, P)
                part = q_parts[r, b % 2, g, :]
                V.scalar_tensor_tensor(part, m[r, :], bq_rep[r, g:g + 1], part.bitcast(f32),
                                       ALU.add, ALU.subtract).then_inc(mi_dve, 1)

            def max_group(b, g):
                if b and g == 0:
                    dve.wait_ge(nmax_split, b)
                for t in range(TT):
                    m = mi_wait(dve, "a", b, g * TT + t)
                    V.tensor_reduce(nmax[:, t, g * GH:(g + 1) * GH], m[:, 0:GK].rearrange("p (h k) -> p h k", k=CTX),
                                    AX.X, ALU.max, negate=True).then_inc(mi_dve, 1)

            def split_max(b):
                dve.wait_ge(mi_dve, read_count(job("a", b, TT * GROUPS - 1)))
                if b:
                    dve.wait_ge(mi_filled, job("mT", b - 1) + 1)
                hi, lo = nmax_parts[:, :, 0:HEADS], nmax_parts[:, :, HEADS:2 * HEADS]
                link(V.tensor_copy(hi, nmax[:, :, :]))
                V.tensor_tensor(lo, nmax[:, :, :], hi.bitcast(f32), ALU.subtract).then_inc(nmax_split, 1)

            def invert_den(b):
                m = mi_wait(dve, "dT", b)
                if b:
                    dve.wait_ge(rden_t_kept, b)
                V.reciprocal(rden[:, :, :], m.rearrange("p (t h d) -> p t h d", h=HEADS, d=DH)[:, :, :, 0]).then_inc(rden_kept, 1)
                dve.wait_ge(rden_kept, b + 1)
                V.tensor_copy(read_mark[:, :], rden[:, 0, 0:1]).then_inc(mi_dve, 1)

            def normalise(b):
                dve.wait_ge(sums_done, CHUNKS * (b + 1))
                dve.wait_ge(mi_act, read_count(job("rT", b)))
                if b:
                    dve.wait_ge(mi_filled, job("y", b - 1) + 1)
                V.tensor_tensor(attnT[:, :], ol[:, 0, :], rden_hd[:, :], ALU.mult).then_inc(attn_kept, 1)

            def residual(b):
                m = mi_wait(dve, "y", b)
                dve.wait_ge(xb_kept, b + 1)
                t0 = b * TT
                V.tensor_tensor(rows[:, t0:t0 + TT, D:2 * D], m.rearrange("p (t d) -> p t d", d=D), xb[:, b % 2],
                                ALU.add).then_inc(mi_dve, 1)
                dve.wait_ge(mi_dve, read_count(job("y", b)))
                stats(b, lambda t: rows[:, t0 + t, D:2 * D], st2, mv2, ln2_stats)

            def keep_logits(b):
                m = mi_wait(dve, "lg", b)
                if b == 0:
                    dve.wait_ge(ld_ffn, 96)
                V.tensor_tensor(lg[:, :, b * TT:(b + 1) * TT], m[:, 0:TT * EXPERTS].rearrange("p (t e) -> p e t", e=EXPERTS),
                                rb_bc[:, :].unsqueeze(2).to_broadcast([P, EXPERTS, TT]), ALU.add).then_inc(mi_dve, 1)

            def choose(r):
                t0, t1 = ROUNDS[r]
                tiles = t1 - t0
                w = EXPERTS * tiles

                def by_e(buf):
                    return buf[:, 0:w].rearrange("p (e t) -> p e t", t=tiles)

                def by_t(buf):
                    return buf[:, 0:w].rearrange("p (e t) -> p t e", t=tiles)

                def over_e(ap):
                    return ap.unsqueeze(1).to_broadcast([P, EXPERTS, tiles])

                dve.wait_ge(mi_dve, read_count(job("lg", t1 // TT - 1)))
                if r:
                    dve.wait_ge(mi_filled, job("rk", r - 1) + 1)
                logit = lg[:, :, t0:t1]
                link(V.tensor_reduce(mx[:, 0:tiles], logit.rearrange("p e t -> p t e"), AX.X, ALU.max))
                link(V.tensor_tensor(by_e(top), logit, over_e(mx[:, 0:tiles]), ALU.is_ge))
                V.tensor_tensor(by_e(ex), logit, over_e(mx[:, 0:tiles]), ALU.subtract).then_inc(shifted, 1)
                link(V.tensor_tensor(by_e(top), by_e(top), rev.unsqueeze(2).to_broadcast([P, EXPERTS, tiles]), ALU.mult))
                link(V.tensor_reduce(den[:, 0:tiles], by_t(top), AX.X, ALU.max))
                link(V.tensor_tensor(by_e(one_hot), by_e(top), over_e(den[:, 0:tiles]), ALU.is_equal))
                V.tensor_tensor_scan(upto[:, 0:w], cs[:, C_RS + EXPERTS * t0:C_RS + EXPERTS * t1], one_hot[:, 0:w], 0.0,
                                     ALU.mult, ALU.add).then_inc(one_hot_kept, 1)
                dve.wait_ge(ex_kept, r + 1)
                link(V.reduce_sum(mx[:, 0:tiles], by_t(ex), AX.X))
                link(V.reciprocal(rows[:, t0:t1, 2 * D], mx[:, 0:tiles]))

            def route(r):
                t0, t1 = ROUNDS[r]
                tiles = t1 - t0
                w = EXPERTS * tiles
                new, old = (r + 1) % 2, r % 2

                def by_e(buf):
                    return buf[:, 0:w].rearrange("p (e t) -> p e t", t=tiles)

                def over_t(ap):
                    return ap.unsqueeze(2).to_broadcast([P, EXPERTS, tiles])

                if r == 0:
                    link(V.memset(total[:, old, :], 0.0))
                    link(V.memset(npages[:, old, :], 0.0))
                    link(V.memset(base[:, :], 0.0))
                    link(V.memset(ends[:, 0, :], 0.0))
                    link(V.memset(page_ex[:, :], 0.0))
                used = ends[:, r, EXPERTS - 1:EXPERTS]
                link(V.tensor_scalar(edge[:, :], npages[:, old, :], float(P), None, ALU.mult))
                m = mi_wait(dve, "rk", r)
                link(V.tensor_tensor(total[:, new, :], m[:, w:w + EXPERTS], total[:, old, :], ALU.add))
                link(V.tensor_tensor(cmp_pg[:, :, :], page_edges.unsqueeze(1).to_broadcast([P, EXPERTS, TILES]),
                                     total[:, new, :].unsqueeze(2).to_broadcast([P, EXPERTS, TILES]), ALU.is_lt))
                V.tensor_tensor(by_e(rank), m[:, 0:w].rearrange("p (e t) -> p e t", t=tiles),
                                over_t(total[:, old, :]), ALU.add).then_inc(mi_dve, 1)
                link(V.reduce_sum(npages[:, new, :], cmp_pg[:, :, :], AX.X))
                dve.wait_ge(mi_dve, read_count(job("rk", r)))
                link(V.tensor_tensor(by_e(fresh_part), by_e(rank), over_t(edge[:, :]), ALU.is_ge))
                link(V.tensor_tensor(fresh[:, :], npages[:, new, :], npages[:, old, :], ALU.subtract))
                link(V.tensor_tensor(by_e(offs), by_e(rank), over_t(base[:, :]), ALU.add))
                link(V.tensor_tensor_scan(ends[:, r + 1, :], ones[:, 0:EXPERTS], fresh[:, :], used, ALU.mult, ALU.add))
                link(V.tensor_tensor(fresh_part[:, 0:w], fresh_part[:, 0:w], one_hot[:, 0:w], ALU.mult))
                link(V.tensor_tensor(move[:, :], ends[:, r + 1, :], npages[:, new, :], ALU.subtract))
                link(V.tensor_tensor(offs[:, 0:w], offs[:, 0:w], one_hot[:, 0:w], ALU.mult))
                link(V.scalar_tensor_tensor(move[:, :], move[:, :], float(P), base[:, :], ALU.mult, ALU.subtract))
                link(V.tensor_tensor(by_e(fresh_part), by_e(fresh_part), over_t(move[:, :]), ALU.mult))
                link(V.tensor_tensor(offs[:, 0:w], offs[:, 0:w], fresh_part[:, 0:w], ALU.add))
                link(V.reduce_sum(den[:, 0:tiles], offs[:, 0:w].rearrange("p (e t) -> p t e", t=tiles), AX.X))
                V.tensor_copy(slot_no[:, t0:t1], den[:, 0:tiles]).then_inc(routed, 1)
                link(V.scalar_tensor_tensor(move[:, :], fresh[:, :], 0.0, move[:, :], ALU.is_gt, ALU.mult))
                link(V.tensor_tensor(base[:, :], base[:, :], move[:, :], ALU.add))
                link(V.tensor_tensor(cmp_ex[:, :, :], ends[:, r + 1, :].unsqueeze(1).to_broadcast([P, PAGES, EXPERTS]),
                                     page_no.unsqueeze(2).to_broadcast([P, PAGES, EXPERTS]), ALU.is_le))
                link(V.reduce_sum(owner[:, :], cmp_ex[:, :, :], AX.X))
                link(V.tensor_scalar(owner[:, :], owner[:, :], float(EXPERTS - 1), None, ALU.min))
                link(V.scalar_tensor_tensor(owner[:, :], page_no, used, owner[:, :], ALU.is_ge, ALU.mult))
                link(V.scalar_tensor_tensor(owner[:, :], page_no, ends[:, r + 1, EXPERTS - 1:EXPERTS], owner[:, :],
                                            ALU.is_lt, ALU.mult))
                link(V.tensor_tensor(page_ex[:, 1:PAGES + 1], page_ex[:, 1:PAGES + 1], owner[:, :], ALU.add))

            V.memset(selr[:, :, :].bitcast(f32), 0.0).then_inc(selr_zero, 1)
            V.memset(nmaxT[:, :, :].bitcast(f32), 0.0).then_inc(selr_zero, 1)
            stats1(0)
            dve.wait_ge(b_kept, 1)
            dve.wait_ge(ld_cst, 16)
            V.tensor_tensor(bk_low[:, :], bk_rep, is_low.to_broadcast([P, GROUPS]), ALU.mult).then_inc(bk_low_kept, 1)
            dve.wait_ge(k_hi_kept, 2 * GROUPS)
            V.scalar_tensor_tensor(k_parts[:, :, :, :].rearrange("p g b k -> p (g b k)"),
                                   k_hi[:, :, :, :].rearrange("p g b k -> p (g b k)").bitcast(f32), sign_low,
                                   k_low_src[:, :, :, :].rearrange("p g b k -> p (g b k)"),
                                   ALU.mult, ALU.add).then_inc(k_kept, 1)
            dve.wait_ge(k_kept, 1)
            for g in range(GROUPS):
                V.tensor_tensor(k_blk[:, 0, g, 0:GK].rearrange("p (h k) -> p h k", k=CTX),
                                k_parts[:, g, 0, :].unsqueeze(1).to_broadcast([P, GH, CTX]),
                                head_mask.unsqueeze(2).to_broadcast([P, GH, CTX]), ALU.mult).then_inc(k_blk_kept, 1)
            for g in range(GROUPS):
                q_low(0, g)
            dve.wait_ge(ld_bias, 64)
            for g in range(GROUPS):
                max_group(0, g)
                m = mi_wait(dve, "v", g)
                if g == 0:
                    V.tensor_tensor(bo2[:, :], m[:, CHUNKS * D:(CHUNKS + 1) * D], bo_bc[:, :], ALU.add).then_inc(bo2_kept, 1)
                keep_values(m, g).then_inc(mi_dve, 1)
            split_max(0)
            stats1(1)
            for b in range(BATCH):
                n = b + 1
                more = n < BATCH
                if more:
                    q_low(n, 0)
                if b:
                    normalise(b - 1)
                    residual(b - 1)
                if more:
                    q_low(n, 1)
                    max_group(n, 0)
                    q_low(n, 2)
                    max_group(n, 1)
                    q_low(n, 3)
                    max_group(n, 2)
                if b + 2 < BATCH:
                    stats1(b + 2)
                if more:
                    max_group(n, 3)
                    split_max(n)
                if b:
                    keep_logits(b - 1)
                invert_den(b)
            choose(0)
            normalise(BATCH - 1)
            residual(BATCH - 1)
            route(0)
            keep_logits(BATCH - 1)
            choose(1)
            route(1)
            V.tensor_copy(page_exi[:, :, 0:2], page_ex[:, 0:2 * STEPS].rearrange("p (i j) -> p i j", j=2)).then_inc(experts_kept, 1)
            V.tensor_copy(page_exi[:, :, 2:4], page_ex[:, 2:2 * STEPS + 2].rearrange("p (i j) -> p i j", j=2)).then_inc(experts_kept, 1)
            dve.wait_ge(experts_kept, 2)

            def keep_page(s, k):
                dve.wait_ge(pgT_done, s + 1)
                V.tensor_copy(pgT[:, k, :], mi[:, k, 0:P]).then_inc(pgT_kept, 1)

            def add_b1(s, k, e):
                dve.wait_ge(up_done, s + 1)
                V.tensor_tensor(hid[:, k, :], sc[:, k, :], b1_bc[:, bass.ds(e * FF, FF)], ALU.add).then_inc(hid_kept, 1)

            def finish(s, k, e):
                dve.wait_ge(down_done, s + 1)
                V.tensor_tensor(y_sb[:, k, :], (sc[:, 2] if k else mi[:, 2])[:, 0:D], b2_bc[:, bass.ds(e * D, D)], ALU.add).then_inc(y_kept, 1)
                if not isinstance(s, int) or s >= 2:
                    dve.wait_ge(written[k], 16 * (s // 2) if isinstance(s, int) else 8 * (s - k))
                rest = pg_rest[:, s, :] if isinstance(s, int) else \
                    pg_rest.rearrange("p s r -> p (s r)")[:, bass.ds(s * REST, REST)]
                V.tensor_copy(gate_tok[:, k, :], rest[:, D:REST]).then_inc(tok_kept, 1)
                dve.wait_ge(y_kept, s + 1)
                dve.wait_ge(tok_kept, s + 1)
                V.scalar_tensor_tensor(out_sb[:, k, :], y_sb[:, k, :], gate_tok[:, k, 0:1], rest[:, 0:D],
                                       ALU.mult, ALU.add).then_inc(out_kept, 1)

            keep_page(0, 0)
            _, e0, e1, _ = load_experts(dve, 0)
            keep_page(1, 1)
            add_b1(0, 0, e0)
            keep_page(2, 0)
            add_b1(1, 1, e1)
            dve.wait_ge(rest_loaded, 16 * len(REST_CUTS))
            finish(0, 0, e0)

            def two_pages(s):
                before_s, of_s, after_s, _ = load_experts(dve, s)
                keep_page(s + 1, 1)
                add_b1(s, 0, of_s)
                finish(s - 1, 1, before_s)
                keep_page(s + 2, 0)
                add_b1(s + 1, 1, after_s)
                finish(s, 0, of_s)

            two_pages(2)
            with dve.Fori(4, PAGES - 1, 2) as s:
                two_pages(s)
            before_s, of_s, _, _ = load_experts(dve, PAGES - 1)
            add_b1(PAGES - 1, 0, of_s)
            finish(PAGES - 2, 1, before_s)
            finish(PAGES - 1, 0, of_s)


def constants():
    import numpy as np
    r = np.arange(P)
    c = np.zeros((P, CC), np.float32)
    c[:, C_ID:C_ID + P] = np.eye(P)
    c[:, C_LT:C_LT + P] = -(r[:, None] >= r[None, :]).astype(np.float32)
    c[:, C_ONE:C_ONE + P] = 1
    c[:, C_HM:C_HM + GH] = (r[:, None] % 32) // DH == np.arange(GH)
    head = (np.arange(CHUNKS)[None, :] * P + r[:, None]) // CTX
    mask = (head[:, :, None] == np.arange(GH)).astype(np.float32)
    c[:, C_MC:C_ON] = np.repeat(mask[:, :, None, :], GROUPS, 2).reshape(P, -1)
    c[:, C_ON:C_REV] = np.repeat(mask, DH, 2).reshape(P, -1)
    c[:, C_REV:C_REV + EXPERTS] = EXPERTS - np.arange(EXPERTS)
    c[:, C_LO] = (r // 32) % 2
    c[:, C_LO + 1] = 1 - 2 * c[:, C_LO]
    for t0, t1 in ROUNDS:
        c[:, C_RS + EXPERTS * t0:C_RS + EXPERTS * t1] = np.tile(np.arange(t1 - t0) > 0, EXPERTS)
    c[:, C_PG:C_PG + TILES] = P * np.arange(TILES)
    c[:, C_SL:C_SL + PAGES] = np.arange(PAGES)
    c[:, C_TOK:C_TOK + TILES] = (P * np.arange(TILES)[None, :] + r[:, None]).astype(np.int32).view(np.float32)
    c[:, C_NH:C_NH + 4] = -0.5
    sel = np.zeros((32, GROUPS, CHUNKS, P), np.float32)
    for g in range(GROUPS):
        for h in range(GH):
            for part in range(2):
                sel[part * HEADS + g * GH + h, g] = mask[:, :, h].T
    return c, sel.reshape(32, GROUPS * CHUNKS, P)


_INS = ['x', 'ctx_1024', 'L0_xattn_Wq', 'L0_xattn_bq', 'L0_xattn_Wk', 'L0_xattn_bk', 'L0_xattn_Wv', 'L0_xattn_bv',
        'L0_xattn_Wo', 'L0_xattn_bo', 'L0_ffn_router_W', 'L0_ffn_router_b', 'L0_ffn_W1', 'L0_ffn_b1', 'L0_ffn_W2',
        'L0_ffn_b2']


def kernel(**inputs):
    import numpy as _np
    import concourse.bacc as _bacc
    from concourse import mybir as _mybir
    from concourse.bass_utils import run_bass_kernel_spmd as _run

    nc = _bacc.Bacc("TRN2", target_bir_lowering=False, num_devices=1)
    cst, sel = constants()
    given = [(n, _np.ascontiguousarray(inputs[n])) for n in _INS] + [("constants", cst), ("selector", sel)]
    arrays, args = {}, []
    for name, a in given:
        arrays[f"in_{name}"] = a
        args.append(nc.dram_tensor(f"in_{name}", a.shape, _mybir.dt.from_np(a.dtype), kind="ExternalInput").ap())
    args.append(nc.dram_tensor("out_0", (BATCH, SEQ, D), _mybir.dt.float32, kind="ExternalOutput").ap())
    layer(nc, *args)
    r = _run(nc, [arrays], core_ids=[0])
    return r.results[0]["out_0"]
```
